# Optimizing a Trainium2 kernel written in Bass

```python
import numpy as np
import jax
import jax.numpy as jnp

def _softmax(x, axis=-1):
    return jax.nn.softmax(x, axis=axis)

def _gelu(x):
    return jax.nn.gelu(x, approximate=True)

def _silu(x):
    return jax.nn.silu(x)

def _sigmoid(x):
    return jax.nn.sigmoid(x)

def _layernorm(x, axis=-1, eps=1e-05):
    m = jnp.mean(x, axis=axis, keepdims=True)
    v = jnp.var(x, axis=axis, keepdims=True)
    return (x - m) / jnp.sqrt(v + eps)

def _scatter_add(tgt, idx, src, axis=0):
    return tgt.at[idx].add(src)

def _segment_sum(src, seg, n):
    return jax.ops.segment_sum(src, seg, n)
kernel_name = 'mk_perceiver_d1_seqx_r4_faea43'

def setup_inputs(seed: int=0):
    np.random.seed(seed)
    _w = jnp.asarray

    def _rec_inputs():
        import jax
        import jax.numpy as jnp
        _rk = jax.random.key(seed)
        x = -0.0002928 + 1 * jax.random.normal(jax.random.fold_in(_rk, 1), (8, 64, 256), jnp.float32)
        _lenS = 64 - jax.random.randint(jax.random.fold_in(_rk, 7), (8,), 0, max(1, 64 // 4) + 1, jnp.int32)
        _lenS2 = 1601 - jax.random.randint(jax.random.fold_in(_rk, 8), (8,), 0, max(1, 1601 // 4) + 1, jnp.int32)
        _ctx_1024P = jax.random.normal(jax.random.fold_in(_rk, 11), (8, 16, 256), jnp.float32)
        _ctx_1024c = jax.random.dirichlet(jax.random.fold_in(_rk, 511), 0.3 * jnp.ones((16,), jnp.float32), (8, 1601))
        _ctx_1024t = jnp.einsum('bsk,bkd->bsd', _ctx_1024c, _ctx_1024P)
        _ctx_1024t = _ctx_1024t * jax.lax.rsqrt(jnp.mean(jnp.square(_ctx_1024t)) + 1e-12) * 0.953939
        ctx_1024 = 4.13588e-05 + 0.999923 * (_ctx_1024t + 0.3 * jax.random.normal(jax.random.fold_in(_rk, 611), (8, 1601, 256), jnp.float32))
        return (x, ctx_1024)
    x, ctx_1024 = _rec_inputs()

    def _L0_xattn_setup():
        import jax, jax.numpy as jnp
        import numpy as np
        DIM = 256
        NUM_HEADS = 16
        DIM_HEAD = 64
        INNER = NUM_HEADS * DIM_HEAD
        SCALE = DIM_HEAD ** (-0.5)

        def _layernorm(x, gamma, beta, eps=1e-05):
            mu = jnp.mean(x, axis=-1, keepdims=True)
            var = jnp.mean(jnp.square(x - mu), axis=-1, keepdims=True)
            return (x - mu) * jax.lax.rsqrt(var + eps) * gamma + beta
        key = jax.random.key(seed)
        ks = jax.random.split(key, 8)
        B, SQ, SK = (2, 512, 1024)
        x = jax.random.normal(ks[0], (B, SQ, DIM), dtype=jnp.float32)
        context = jax.random.normal(ks[1], (B, SK, DIM), dtype=jnp.float32)
        ln_gamma = jnp.ones((DIM,), jnp.float32)
        ln_beta = jnp.zeros((DIM,), jnp.float32)
        w_q = jax.random.normal(ks[2], (DIM, INNER), dtype=jnp.float32) / np.sqrt(DIM)
        w_kv = jax.random.normal(ks[3], (DIM, 2 * INNER), dtype=jnp.float32) / np.sqrt(DIM)
        w_out = jax.random.normal(ks[4], (INNER, DIM), dtype=jnp.float32) / np.sqrt(INNER)
        b_out = jnp.zeros((DIM,), jnp.float32)
        gate = jnp.array([0.5], jnp.float32)
        return {'x': x, 'context': context, 'ln_gamma': ln_gamma, 'ln_beta': ln_beta, 'w_q': w_q, 'w_kv': w_kv, 'w_out': w_out, 'b_out': b_out, 'gate': gate}
    _L0_xattn_all = _L0_xattn_setup()
    _L0_xattn_in = {k: v for k, v in _L0_xattn_all.items() if k in ('ln_gamma', 'ln_beta', 'w_q', 'w_kv', 'w_out', 'b_out', 'gate')}
    del _L0_xattn_all

    def _L0_attn_setup():
        import jax, jax.numpy as jnp
        import numpy as np
        B, N, QD = (4, 1024, 256)
        HEADS, DIM_HEAD = (8, 64)
        HID = HEADS * DIM_HEAD
        SCALE = DIM_HEAD ** (-0.5)
        key = jax.random.key(seed)
        ks = jax.random.split(key, 6)
        s_in = 1.0 / np.sqrt(QD)
        s_h = 1.0 / np.sqrt(HID)
        return {'x': jax.random.normal(ks[0], (B, N, QD), dtype=jnp.float32), 'Wq': jax.random.uniform(ks[1], (QD, HID), jnp.float32, -s_in, s_in), 'Wk': jax.random.uniform(ks[2], (QD, HID), jnp.float32, -s_in, s_in), 'Wv': jax.random.uniform(ks[3], (QD, HID), jnp.float32, -s_in, s_in), 'Wo': jax.random.uniform(ks[4], (HID, QD), jnp.float32, -s_h, s_h), 'bo': jax.random.uniform(ks[5], (QD,), jnp.float32, -s_h, s_h)}
    _L0_attn_all = _L0_attn_setup()
    _L0_attn_in = {k: v for k, v in _L0_attn_all.items() if k in ('Wq', 'Wk', 'Wv', 'Wo', 'bo')}
    del _L0_attn_all

    def _L0_ffn_setup():
        import jax, jax.numpy as jnp
        import numpy as np
        N_EMBD = 256
        NUM_EXPERTS = 8
        TOP_K = 2
        D_FF = 4 * N_EMBD
        B, S = (4, 512)
        key = jax.random.key(seed)
        ks = jax.random.split(key, 7)
        scale = lambda fan_in: 1.0 / np.sqrt(fan_in)
        x = jax.random.normal(ks[0], (B, S, N_EMBD), dtype=jnp.float32)
        W_router = jax.random.normal(ks[1], (N_EMBD, NUM_EXPERTS), dtype=jnp.float32) * scale(N_EMBD)
        b_router = jnp.zeros((NUM_EXPERTS,), dtype=jnp.float32)
        W1 = jax.random.normal(ks[2], (NUM_EXPERTS, N_EMBD, D_FF), dtype=jnp.float32) * scale(N_EMBD)
        b1 = jnp.zeros((NUM_EXPERTS, D_FF), dtype=jnp.float32)
        W2 = jax.random.normal(ks[3], (NUM_EXPERTS, D_FF, N_EMBD), dtype=jnp.float32) * scale(D_FF)
        b2 = jnpp = jnp.zeros((NUM_EXPERTS, N_EMBD), dtype=jnp.float32)
        return {'x': x, 'W_router': W_router, 'b_router': b_router, 'W1': W1, 'b1': b1, 'W2': W2, 'b2': b2}
    _L0_ffn_all = _L0_ffn_setup()
    _L0_ffn_in = {k: v for k, v in _L0_ffn_all.items() if k in ('W_router', 'b_router', 'W1', 'b1', 'W2', 'b2')}
    del _L0_ffn_all
    return {'x': x, 'ctx_1024': ctx_1024, 'L0_xattn_ln_gamma': _L0_xattn_in['ln_gamma'], 'L0_xattn_ln_beta': _L0_xattn_in['ln_beta'], 'L0_xattn_w_q': _L0_xattn_in['w_q'], 'L0_xattn_w_kv': _L0_xattn_in['w_kv'], 'L0_xattn_w_out': _L0_xattn_in['w_out'], 'L0_xattn_b_out': _L0_xattn_in['b_out'], 'L0_xattn_gate': _L0_xattn_in['gate'], 'L0_attn_Wq': _L0_attn_in['Wq'], 'L0_attn_Wk': _L0_attn_in['Wk'], 'L0_attn_Wv': _L0_attn_in['Wv'], 'L0_attn_Wo': _L0_attn_in['Wo'], 'L0_attn_bo': _L0_attn_in['bo'], 'L0_ffn_W_router': _L0_ffn_in['W_router'], 'L0_ffn_b_router': _L0_ffn_in['b_router'], 'L0_ffn_W1': _L0_ffn_in['W1'], 'L0_ffn_b1': _L0_ffn_in['b1'], 'L0_ffn_W2': _L0_ffn_in['W2'], 'L0_ffn_b2': _L0_ffn_in['b2']}

def reference(x, ctx_1024, L0_xattn_ln_gamma, L0_xattn_ln_beta, L0_xattn_w_q, L0_xattn_w_kv, L0_xattn_w_out, L0_xattn_b_out, L0_xattn_gate, L0_attn_Wq, L0_attn_Wk, L0_attn_Wv, L0_attn_Wo, L0_attn_bo, L0_ffn_W_router, L0_ffn_b_router, L0_ffn_W1, L0_ffn_b1, L0_ffn_W2, L0_ffn_b2):
    import jax
    import jax.numpy as jnp

    def _L0_xattn_ref(x, context, ln_gamma, ln_beta, w_q, w_kv, w_out, b_out, gate):
        import jax, jax.numpy as jnp
        import numpy as np
        DIM = 256
        NUM_HEADS = 16
        DIM_HEAD = 64
        INNER = NUM_HEADS * DIM_HEAD
        SCALE = DIM_HEAD ** (-0.5)

        def _layernorm(x, gamma, beta, eps=1e-05):
            mu = jnp.mean(x, axis=-1, keepdims=True)
            var = jnp.mean(jnp.square(x - mu), axis=-1, keepdims=True)
            return (x - mu) * jax.lax.rsqrt(var + eps) * gamma + beta
        B, SQ, _ = x.shape
        SK = context.shape[1]
        xn = _layernorm(x, ln_gamma, ln_beta)
        q = (xn @ w_q).reshape(B, SQ, NUM_HEADS, DIM_HEAD)
        kv = context @ w_kv
        k, v = jnp.split(kv, 2, axis=-1)
        k = k.reshape(B, SK, NUM_HEADS, DIM_HEAD)
        v = v.reshape(B, SK, NUM_HEADS, DIM_HEAD)
        scores = jnp.einsum('bqhd,bkhd->bhqk', q * SCALE, k)
        attn = jax.nn.softmax(scores, axis=-1)
        out = jnp.einsum('bhqk,bkhd->bqhd', attn, v).reshape(B, SQ, INNER)
        out = out @ w_out + b_out
        return out * jnp.tanh(gate[0])

    def _L0_attn_ref(x, Wq, Wk, Wv, Wo, bo):
        import jax, jax.numpy as jnp
        import numpy as np
        B, N, QD = (4, 1024, 256)
        HEADS, DIM_HEAD = (8, 64)
        HID = HEADS * DIM_HEAD
        SCALE = DIM_HEAD ** (-0.5)
        b, n, _ = x.shape
        q = x @ Wq
        k = x @ Wk
        v = x @ Wv

        def split_heads(t):
            return t.reshape(b, n, HEADS, DIM_HEAD).transpose(0, 2, 3, 1)
        q = split_heads(q)
        k = split_heads(k)
        v = split_heads(v)
        q = jax.nn.softmax(q, axis=-2) * SCALE
        k = jax.nn.softmax(k, axis=-1)
        context = jnp.einsum('bhdn,bhen->bhde', k, v)
        out = jnp.einsum('bhde,bhdn->bhen', context, q)
        out = out.transpose(0, 3, 1, 2).reshape(b, n, HID)
        return out @ Wo + bo

    def _L0_ffn_ref(x, W_router, b_router, W1, b1, W2, b2):
        import jax, jax.numpy as jnp
        import numpy as np
        N_EMBD = 256
        NUM_EXPERTS = 8
        TOP_K = 2
        D_FF = 4 * N_EMBD
        B, S = (4, 512)
        Bv, Sv, D = x.shape
        flat_x = x.reshape(-1, D)
        T = flat_x.shape[0]
        logits = flat_x @ W_router + b_router
        top_vals, top_idx = jax.lax.top_k(logits, TOP_K)
        neg_inf = jnp.full_like(logits, -jnp.inf)
        sparse_logits = neg_inf.at[jnp.arange(T)[:, None], top_idx].set(top_vals)
        router_weights = jax.nn.softmax(sparse_logits, axis=-1)
        final_output = jnp.zeros_like(flat_x)
        for e in range(NUM_EXPERTS):
            expert_mask = jnp.any(top_idx == e, axis=-1)
            h = jax.nn.relu(flat_x @ W1[e] + b1[e])
            y = h @ W2[e] + b2[e]
            w = router_weights[:, e] * expert_mask.astype(x.dtype)
            final_output = final_output + y * w[:, None]
        return final_output.reshape(Bv, Sv, D)
    x = x + _L0_xattn_ref(_layernorm(x, axis=-1), ctx_1024, L0_xattn_ln_gamma, L0_xattn_ln_beta, L0_xattn_w_q, L0_xattn_w_kv, L0_xattn_w_out, L0_xattn_b_out, L0_xattn_gate)
    x = x + _L0_attn_ref(_layernorm(x, axis=-1), L0_attn_Wq, L0_attn_Wk, L0_attn_Wv, L0_attn_Wo, L0_attn_bo)
    x = x + _L0_ffn_ref(_layernorm(x, axis=-1), L0_ffn_W_router, L0_ffn_b_router, L0_ffn_W1, L0_ffn_b1, L0_ffn_W2, L0_ffn_b2)
    return x

_drawn_inputs = setup_inputs


def setup_inputs(seed=0):
    import zlib

    import numpy as np

    out = dict(_drawn_inputs(seed))
    spreads = {'L0_xattn_ln_gamma': (1.0, 0.2),
     'L0_xattn_ln_beta': (0.0, 0.1),
     'L0_xattn_b_out': (0.0, 0.1),
     'L0_ffn_b_router': (0.0, 0.1),
     'L0_ffn_b1': (0.0, 0.1),
     'L0_ffn_b2': (0.0, 0.1)}
    factors = {'L0_attn_Wq': 5.48, 'L0_attn_Wk': 5.473}
    for name, (base, spread) in spreads.items():
        noise = np.random.default_rng([zlib.crc32(name.encode()), seed]).standard_normal(out[name].shape)
        drawn = base * np.exp(spread * noise) if base else spread * noise
        out[name] = jnp.asarray(drawn.astype(out[name].dtype))
    for name, factor in factors.items():
        out[name] = (out[name] * factor).astype(out[name].dtype)
    return out
```

```python
from contextlib import ExitStack

import concourse.bass as bass
from concourse import mybir

F32 = mybir.dt.float32
F32R = mybir.dt.float32r
U32 = mybir.dt.uint32
ALU = mybir.AluOpType
ACT = mybir.ActivationFunctionType
AX = mybir.AxisListType

P = 128
B, Q, D = 8, 64, 256
S = 1601
SP = S + 1
H, DH = 16, 64
TOK = B * Q
MT = TOK // P
DT = D // P
TPB = H * Q // P
NT = B * TPB
SJ = (S + P - 1) // P
SL = S - (SJ - 1) * P
SG = (SJ + 3) // 4
CW = 400
NC = 4
CWID = [CW, CW, CW, SP - 3 * CW]
CREAL = [CW, CW, CW, S - 3 * CW]
NCN = (SJ + 1) // 2
NCT = 2 * NC
PAIR = 2 * TPB
LH, LD = 8, 64
HID = LH * LD
HP = HID // P
NE, FF = 8, 1024
FT = FF // P
EPS = 1e-5


def build(nc, x, ctx_n, ctx_t, gamma, beta, w_q, w_kt, w_v, w_out, b_out, gate, Wq, Wk, Wv, Wo, bo,
          W_router, b_router, W1, b1, W2, b2, out):
    with ExitStack() as es:
        def sb(name, shape, dt=F32):
            return es.enter_context(nc.sbuf_tensor(name, shape, dt))

        def sem(name):
            return es.enter_context(nc.semaphore(name))

        qk_dram = nc.dram_tensor("qk_scratch", (NT, P, DT * P), F32, kind="Internal").ap()

        x_sb = sb("x_sb", [P, MT, D])
        ident = sb("ident", [P, P])
        gamma_b = sb("gamma_b", [P, D])
        beta_b = sb("beta_b", [P, D])
        bout_b = sb("bout_b", [P, D])
        bo_b = sb("bo_b", [P, D])
        tg = sb("tg", [P, 2])
        zero = sb("zero", [P, 1])
        stats = sb("stats", [P, MT, 6])
        mv = sb("mv", [P, MT, 2])
        sd = sb("sd", [P, MT])
        rstd = sb("rstd", [P, MT])
        wv_sb = sb("wv_sb", [P, DT, H * DH])
        wout_sb = sb("wout_sb", [P, TPB, D])
        lw_sb = sb("lw_sb", [P, 3, DT, HID])
        wo_sb = sb("wo_sb", [P, HP, D])
        wr_sb = sb("wr_sb", [P, DT, NE])
        br_b = sb("br_b", [P, NE])
        stage = sb("stage", [P, 2, B, 2 * P])
        xn = stage[:, 1, 0:B // 2, :]
        xnT = stage[:, 1, B // 2:B, :].rearrange("p (t b) f -> p t (b f)", t=DT)
        loop_scope = ExitStack()

        def lsb(name, shape, dt=F32):
            return loop_scope.enter_context(nc.sbuf_tensor(name, shape, dt))

        ct_hi = lsb("ct_hi", [P, 2, DT, SP], F32R)
        ct_lo = lsb("ct_lo", [P, 2, DT, SP], F32R)
        cn = lsb("cn", [P, 2, SJ, 2 * D], F32R)
        ct_raw = lsb("ct_raw", [P, 2, CWID[3]])
        cn_raw = lsb("cn_raw", [P, 2, 2, D])
        qk_raw = lsb("qk_raw", [P, 2, DT * P])
        qk_hi = lsb("qk_hi", [P, 2, DT * P], F32R)
        qk_lo = lsb("qk_lo", [P, 2, DT * P], F32R)
        nmax = lsb("nmax", [P, 2])
        mx2 = lsb("mx2", [P, 2, 2])
        esum = lsb("esum", [P, 2, 2])
        tsum = lsb("tsum", [P, 2])
        rsum = lsb("rsum", [P, 2])
        u_b = lsb("u_b", [P, D])
        u_sb = lsb("u_sb", [P, D])
        ut_sb = lsb("ut_sb", [P, DT, P])
        pro_scope = ExitStack()
        wq_sb = pro_scope.enter_context(nc.sbuf_tensor("wq_sb", [P, DT, H * DH], F32))
        wkt_sb = pro_scope.enter_context(nc.sbuf_tensor("wkt_sb", [P, TPB, D], F32))
        qT = pro_scope.enter_context(nc.sbuf_tensor("qT", [P, TPB, TOK], F32))
        pro_scope.close()
        oT = lsb("oT", [P, TPB, TOK])
        prob = stage[:].rearrange("p s b f -> p (s b f)")[:, 0:S]
        pt_hi = lsb("pt_hi", [P, SJ, P], F32R)
        pt_lo = lsb("pt_lo", [P, SJ, P], F32R)
        loop_scope.close()
        tail = ExitStack()

        def tsb(name, shape, dt=F32):
            return tail.enter_context(nc.sbuf_tensor(name, shape, dt))

        w1_hi = tsb("w1_hi", [P, 2, DT, FF], F32R)
        w1_lo = tsb("w1_lo", [P, 2, DT, FF], F32R)
        w2_sp = tsb("w2_sp", [P, 2, FT, 2 * D], F32R)
        x1 = tsb("x1", [P, MT, D])
        xa = tsb("xa", [P, MT, D])
        ln_out = stage[:, 1, B // 2:B, :]
        lnT = tsb("lnT", [P, DT, TOK])
        lnT_hi = tsb("lnT_hi", [P, DT, TOK], F32R)
        lnT_lo = tsb("lnT_lo", [P, DT, TOK], F32R)
        lin = ExitStack()

        def nsb(name, shape, dt=F32):
            return lin.enter_context(nc.sbuf_tensor(name, shape, dt))

        ke = nsb("ke", [P, HP, TOK])
        kn = nsb("kn", [P, MT, HID])
        qe = nsb("qe", [P, MT, HID])
        lqT = nsb("lqT", [P, HP, TOK])
        v_sb = nsb("v_sb", [P, MT, HID])
        cbd = nsb("cbd", [P, B, HP, P])
        lo_T = stage[:, 0, :, :].rearrange("p (t b) f -> p t (b f)", t=HP)
        bmask = nsb("bmask", [P, P])
        lmax = nsb("lmax", [P, 2, MT, 8])
        lsum = nsb("lsum", [P, 2, MT, 8])
        lrec = nsb("lrec", [P, 2, MT, 8])
        lin.close()
        w1_raw = tsb("w1_raw", [P, 2, DT, FF])
        w2_raw = tsb("w2_raw", [P, 2, FT, D])
        b1_sb = tsb("b1_sb", [P, NE, FT])
        b2_sb = tsb("b2_sb", [NE, D])
        h_f = stage[:, 1, 0:B // 2, :].rearrange("p (t b) f -> p t (b f)", t=2)
        h_hi = tsb("h_hi", [P, FT, TOK], F32R)
        h_lo = tsb("h_lo", [P, FT, TOK], F32R)
        logit = tsb("logit", [P, MT, NE])
        top = tsb("top", [P, MT, 8])
        topi = tsb("topi", [P, MT, 8], U32)
        topf = tsb("topf", [P, MT, 2])
        tdiff = tsb("tdiff", [P, MT])
        texp = tsb("texp", [P, MT])
        tw = tsb("tw", [P, MT, 2])
        sel = tsb("sel", [P, MT, NE])
        gw = tsb("gw", [P, MT, NE])
        gwT = lnT[0:NE, 0, :]
        eidx = tsb("eidx", [P, NE])
        tail.close()

        scp = es.enter_context(nc.psum_tensor("scp", [P, NC, 512], F32))
        trp = [es.enter_context(nc.psum_tensor(f"trp{i}", [P, 512], F32)) for i in range(2)]
        up = es.enter_context(nc.psum_tensor("up", [P, 512], F32))
        wp = es.enter_context(nc.psum_tensor("wp", [P, 512], F32))

        x_in = sem("x_in")
        small_in = sem("small_in")
        pw_in = sem("pw_in")
        tw_in = sem("tw_in")
        ctraw_in = [sem(f"ctraw_in{i}") for i in range(2)]
        cnraw_in = [sem(f"cnraw_in{i}") for i in range(2)]
        qkraw_in = [sem(f"qkraw_in{i}") for i in range(2)]
        qk_out = [sem(f"qk_out{i}") for i in range(2)]
        ident_ok = sem("ident_ok")
        pool_step = sem("pool_step")
        split_hi = sem("split_hi")
        ct_ready = sem("ct_ready")
        cn_ready = sem("cn_ready")
        qk_ready = sem("qk_ready")
        dve_step = sem("dve_step")
        var_ok = sem("var_ok")
        sd_ok = sem("sd_ok")
        xn_ok = sem("xn_ok")
        pro_tr = sem("pro_tr")
        pro_trc = sem("pro_trc")
        pro_q = sem("pro_q")
        pro_qc = sem("pro_qc")
        pro_k = sem("pro_k")
        pro_kc_act = sem("pro_kc_act")
        pro_kc_dve = sem("pro_kc_dve")
        scores_ok = sem("scores_ok")
        pmax_ok = sem("pmax_ok")
        nmax_ok = sem("nmax_ok")
        exp_ok = sem("exp_ok")
        tr_ok = sem("tr_ok")
        hi_ok = sem("hi_ok")
        lo_ok = sem("lo_ok")
        rsum_ok = sem("rsum_ok")
        tsum_ok = sem("tsum_ok")
        pv_ok = sem("pv_ok")
        ub_ok = sem("ub_ok")
        u_ok = sem("u_ok")
        ut_ok = sem("ut_ok")
        utc_ok = sem("utc_ok")
        wv_ok = sem("wv_ok")
        o_ok = sem("o_ok")
        tanh_ok = sem("tanh_ok")
        tp = sem("tp")
        ta = sem("ta")
        tv = sem("tv")
        tq = sem("tq")
        wraw_in = [sem(f"wraw_in{i}") for i in range(2)]
        w_ready = sem("w_ready")
        h_ok = sem("h_ok")
        hf_ok = sem("hf_ok")
        hh_ok = sem("hh_ok")
        hl_ok = sem("hl_ok")
        y_ok = sem("y_ok")
        yc_ok = sem("yc_ok")
        y_stage = sem("y_stage")
        stored = sem("stored")

        def fixed(v):
            return isinstance(v, int) and v <= 0

        def wait(eng, s, v):
            if not fixed(v):
                eng.wait_ge(s, v)

        def hbank(f):
            return [trp[0], trp[1], up, wp][f % 4][:]

        def b1_ap(i, s, f):
            if isinstance(i, int):
                e = i * 2 + s
                return b1_sb[:, e, f:f + 1]
            return b1_sb[:].rearrange("p e f -> p (e f)")[:, bass.ds(i * (2 * FT) + (s * FT + f), 1)]

        block = es.enter_context(nc.Block())

        @block.sync
        def _(sp):
            for m in range(MT):
                sp.dma_start(x_sb[:, m, :], x[P * m:P * (m + 1), :]).then_inc(x_in, 16)
            sp.dma_start(gamma_b[:], gamma.partition_broadcast(P)).then_inc(small_in, 16)
            sp.dma_start(beta_b[:], beta.partition_broadcast(P)).then_inc(small_in, 16)
            sp.dma_start(wq_sb[:], w_q.rearrange("(t p) n -> p t n", p=P)).then_inc(pw_in, 16)
            sp.dma_start(wkt_sb[:], w_kt.rearrange("(t p) n -> p t n", p=P)).then_inc(pw_in, 16)

            def load_ct(b, i, par, k):
                u = NCT * par + k
                wait(sp, ct_ready, i * (2 * NCT) + u - 1)
                dt, c = k // NC, k % NC
                sp.dma_start(ct_raw[:, u % 2, 0:CREAL[c]],
                             ctx_t[b, P * dt:P * (dt + 1), CW * c:CW * c + CREAL[c]]).then_inc(ctraw_in[u % 2], 16)

            def load_cn(b, i, par, k):
                u = NCN * par + k
                wait(sp, cn_ready, i * (2 * NCN) + u - 1)
                if k < NCN - 1:
                    src = ctx_n[b, 2 * P * k:2 * P * (k + 1), :].rearrange("(j p) d -> p j d", p=P)
                    sp.dma_start(cn_raw[:, u % 2, :, :], src).then_inc(cnraw_in[u % 2], 16)
                else:
                    sp.dma_start(cn_raw[0:SL, u % 2, 0, :], ctx_n[b, P * (SJ - 1):S, :]).then_inc(cnraw_in[u % 2], 16)

            def load_qk(n, slot, nn):
                wait(sp, qk_ready, nn - 1)
                sp.dma_start(qk_raw[:, slot, :], qk_dram[n, :, :]).then_inc(qkraw_in[slot], 16)

            for k in range(NCT):
                load_ct(0, 0, 0, k)
                if k < NCN:
                    load_cn(0, 0, 0, k)
            sp.dma_start(wv_sb[:], w_v.rearrange("(t p) n -> p t n", p=P)).then_inc(tw_in, 16)
            sp.dma_start(wout_sb[:], w_out.rearrange("(t p) n -> p t n", p=P)).then_inc(tw_in, 16)
            for i, w in enumerate((Wq, Wk, Wv)):
                sp.dma_start(lw_sb[:, i, :, :], w.rearrange("(t p) n -> p t n", p=P)).then_inc(tw_in, 16)
            sp.dma_start(wo_sb[:], Wo.rearrange("(t p) n -> p t n", p=P)).then_inc(tw_in, 16)
            sp.dma_start(wr_sb[:], W_router.rearrange("(t p) n -> p t n", p=P)).then_inc(tw_in, 16)
            sp.dma_start(br_b[:], b_router.partition_broadcast(P)).then_inc(tw_in, 16)
            sp.dma_start(bout_b[:], b_out.partition_broadcast(P)).then_inc(tw_in, 16)
            sp.dma_start(bo_b[:], bo.partition_broadcast(P)).then_inc(tw_in, 16)
            sp.dma_start(tg[:, 0:1], gate.partition_broadcast(P)).then_inc(tw_in, 16)
            qk_v = qk_dram.rearrange("(b t) p f -> t p b f", t=TPB)
            for t in range(TPB):
                sp.wait_ge(pro_kc_act, 2 * (t + 1))
                sp.wait_ge(pro_kc_dve, 2 * (t + 1))
                sp.dma_start(qk_v[t], stage[:, t % 2, :, :]).then_inc(qk_out[t % 2], 16)
            for i in range(2):
                sp.wait_ge(qk_out[i], 16 * TPB // 2)
            load_qk(0, 0, 0)
            load_qk(1, 1, 1)

            def feed(b, i, par):
                for k in range(TPB):
                    n = (b - 1) * TPB + k + 2
                    load_qk(n, k % 2, n)
                    load_ct(b, i, par, k)
                    if k >= 1:
                        load_cn(b, i, par, k - 1)

            feed(1, 0, 1)
            with sp.Fori(1, B // 2) as i:
                feed(i * 2, i, 0)
                feed(i * 2 + 1, i, 1)
            for n in range(NT - TPB + 2, NT):
                load_qk(n, n % 2, n)

            sp.wait_ge(tp, LIN_PE)
            sp.wait_ge(tv, LIN_DVE)
            sp.dma_start(b1_sb[:], b1).then_inc(small_in, 16)
            sp.dma_start(b2_sb[:], b2).then_inc(small_in, 16)

            def load_expert(e, i, s):
                wait(sp, w_ready, (i * 2 + s - 1) * 3)
                sp.dma_start(w1_raw[:, s, :, :], W1[e].rearrange("(t p) n -> p t n", p=P)).then_inc(wraw_in[s], 16)
                sp.dma_start(w2_raw[:, s, :, :], W2[e].rearrange("(t p) n -> p t n", p=P)).then_inc(wraw_in[s], 16)

            load_expert(0, 0, 0)
            load_expert(1, 0, 1)
            with sp.Fori(1, NE // 2) as i:
                load_expert(i * 2, i, 0)
                load_expert(i * 2 + 1, i, 1)
            for m in range(MT):
                sp.wait_ge(yc_ok, (NE - 1) * MT + m + 1)
                sp.dma_start(out[P * m:P * (m + 1), :], xa[:, m, :]).then_inc(stored, 16)
            sp.wait_ge(stored, 16 * MT)

        @block.gpsimd
        def _(pool):
            steps = [0]

            def link(ins):
                steps[0] += 1
                ins.then_inc(pool_step, 1)
                pool.wait_ge(pool_step, steps[0])

            link(pool.memset(ident[:], 0.0))
            link(pool.memset(zero[:], 0.0))
            pool.affine_select(out=ident[:], in_=ident[:], compare_op=ALU.not_equal, fill=1.0, base=0,
                               pattern=[[-1, P]], channel_multiplier=1).then_inc(ident_ok, 1)
            for t in (ct_hi, ct_lo):
                for par in range(2):
                    pool.memset(t[:, par, :, S:SP].bitcast(F32), 0.0)

            def split(raw, hi, lo, hi_count, done):
                z = zero[0:raw.shape[0], :]
                for _ in range(len(raw.shape) - 2):
                    z = z.unsqueeze(1)
                pool.tensor_tensor(hi, raw, z.broadcast_to(tuple(raw.shape)), ALU.add).then_inc(split_hi, 1)
                pool.wait_ge(split_hi, hi_count + 1)
                pool.tensor_tensor(lo, raw, hi.bitcast(F32), ALU.subtract).then_inc(done, 1)

            def split_ct(b, i, par, k, hc):
                u = NCT * par + k
                pool.wait_ge(ctraw_in[u % 2], 16 * (i * NCT + u // 2 + 1))
                dt, c = k // NC, k % NC
                cs = slice(CW * c, CW * c + CREAL[c])
                split(ct_raw[:, u % 2, 0:CREAL[c]], ct_hi[:, par, dt, cs], ct_lo[:, par, dt, cs], hc, ct_ready)

            def split_cn(b, i, par, k, hc):
                u = NCN * par + k
                pool.wait_ge(cnraw_in[u % 2], 16 * (i * NCN + u // 2 + 1))
                if k < NCN - 1:
                    js = slice(2 * k, 2 * k + 2)
                    split(cn_raw[:, u % 2, :, :], cn[:, par, js, 0:D], cn[:, par, js, D:2 * D], hc, cn_ready)
                else:
                    split(cn_raw[0:SL, u % 2, 0, :], cn[0:SL, par, SJ - 1, 0:D], cn[0:SL, par, SJ - 1, D:2 * D],
                          hc, cn_ready)

            def split_qk(slot, nn, hc):
                pool.wait_ge(qkraw_in[slot], (nn - slot) * 8 + 16)
                wait(pool, scores_ok, (nn - 1) * 2)
                split(qk_raw[:, slot, :], qk_hi[:, slot, :], qk_lo[:, slot, :], hc, qk_ready)

            hc = 0
            for k in range(NCT):
                split_ct(0, 0, 0, k, hc)
                hc += 1
                if k < NCN:
                    split_cn(0, 0, 0, k, hc)
                    hc += 1
            split_qk(0, 0, hc)
            PER = NCT + NCN + TPB
            hc0 = hc + 1

            def feed(b, i, par, hc):
                for k in range(TPB):
                    n = (b - 1) * TPB + k + 1
                    split_qk((k + 1) % 2, n, hc)
                    hc = hc + 1
                    if k == 0:
                        wait(pool, scores_ok, (b - 1) * (2 * TPB))
                    split_ct(b, i, par, k, hc)
                    hc = hc + 1
                    if k == 1:
                        wait(pool, pv_ok, (b - 1) * TPB)
                    if k >= 1:
                        split_cn(b, i, par, k - 1, hc)
                        hc = hc + 1

            feed(1, 0, 1, hc0)
            with pool.Fori(1, B // 2) as i:
                feed(i * 2, i, 0, i * (2 * PER) + (hc0 - PER))
                feed(i * 2 + 1, i, 1, i * (2 * PER) + hc0)
            hc = hc0 + (B - 1) * PER
            for n in range(NT - TPB + 1, NT):
                split_qk(n % 2, n, hc)
                hc += 1

            pool.wait_ge(tp, OUT_PE)
            pool.iota(eidx[:], pattern=[[1, NE]], base=0, channel_multiplier=0,
                      allow_small_or_imprecise_dtypes=True).then_inc(tq, 1)
            hc_e = hc

            def split_expert(i, s, hc):
                pool.wait_ge(wraw_in[s], 32 * (i + 1))
                wait(pool, y_ok, (i * 2 + s - 1) * FT)
                for dt in range(DT):
                    split(w1_raw[:, s, dt, :], w1_hi[:, s, dt, :], w1_lo[:, s, dt, :], hc + dt, w_ready)
                split(w2_raw[:, s, :, :], w2_sp[:, s, :, 0:D], w2_sp[:, s, :, D:2 * D], hc + DT, w_ready)

            split_expert(0, 0, hc_e)
            split_expert(0, 1, hc_e + 3)
            with pool.Fori(1, NE // 2) as i:
                split_expert(i, 0, i * 6 + hc_e)
                split_expert(i, 1, i * 6 + (hc_e + 3))

        @block.scalar
        def _(act):
            for r in range(2):
                act.wait_ge(var_ok, r + 1)
                act.activation(sd[:], mv[:, :, 1], ACT.Sqrt).then_inc(sd_ok, 1)
            for dt in range(DT):
                act.wait_ge(pro_tr, dt + 1)
                act.activation(xnT[:, dt, :], trp[dt][:], ACT.Copy).then_inc(pro_trc, 1)
            for t in range(TPB):
                act.wait_ge(pro_q, t + 1)
                act.activation(qT[:, t, :], scp[:, t % NC, :], ACT.Copy, scale=float(DH) ** -0.5).then_inc(pro_qc, 1)
            for t in range(TPB):
                if t >= 2:
                    act.wait_ge(qk_out[t % 2], 16 * (t // 2))
                for dt in range(DT):
                    act.wait_ge(pro_k, DT * t + dt + 1)
                    act.activation(stage[:, t % 2, :, dt * P:dt * P + Q],
                                   scp[:, 2 * dt, :].rearrange("p (b q) -> p b q", q=Q),
                                   ACT.Copy).then_inc(pro_kc_act, 1)

            def take_u_lo(m, slot):
                act.wait_ge(pv_ok, m + 1)
                act.wait_ge(rsum_ok, m + 1)
                act.activation(u_b[:], up[:, D:2 * D], ACT.Copy, scale=rsum[:, slot:slot + 1]).then_inc(ub_ok, 1)

            def take_hi(m, g):
                j0, j1 = 4 * g, min(4 * g + 4, SJ)
                act.wait_ge(tr_ok, m * SG + g + 1)
                if g == 0:
                    wait(act, pv_ok, m)
                if j1 < SJ:
                    act.activation(pt_hi[:, j0:j1, :], trp[g % 2][:].rearrange("p (j q) -> p j q", q=P),
                                   ACT.Copy).then_inc(hi_ok, 1)
                else:
                    act.activation(pt_hi[0:SL, j0, :], trp[g % 2][0:SL, 0:P], ACT.Copy).then_inc(hi_ok, 1)

            def take_ut(m):
                act.wait_ge(ut_ok, m + 1)
                wait(act, wv_ok, m)
                act.activation(ut_sb[:], wp[:, 0:D].rearrange("p (t q) -> p t q", q=P), ACT.Copy).then_inc(utc_ok, 1)

            def exps(n, slot):
                act.wait_ge(nmax_ok, n + 1)
                wait(act, tr_ok, n * SG)
                act.activation(prob[:, 0:3 * CW].rearrange("p (c w) -> p c w", w=CW), scp[:, 0:3, 0:CW], ACT.Exp,
                               bias=nmax[:, slot:slot + 1], accum_out=esum[:, slot, 0:1]).then_inc(exp_ok, 1)
                act.activation(prob[:, 3 * CW:S], scp[:, 3, 0:CREAL[3]], ACT.Exp,
                               bias=nmax[:, slot:slot + 1], accum_out=esum[:, slot, 1:2]).then_inc(exp_ok, 1)

            def step(n, u, first=False, scores=True, probs=True):
                lag1 = probs and not (first and u < 1)
                lag2 = not (first and u < 2)
                if lag2:
                    take_u_lo(n - 2, u % 2)
                if lag1:
                    take_hi(n - 1, 0)
                    take_hi(n - 1, 1)
                if lag2:
                    take_ut(n - 2)
                if lag1:
                    take_hi(n - 1, 2)
                    take_hi(n - 1, 3)
                if scores:
                    exps(n, u % 2)

            for u in range(PAIR):
                step(u, u, first=True)
            with act.Fori(1, NT // PAIR) as i:
                for u in range(PAIR):
                    step(i * PAIR + u, u)
            step(NT, 0, scores=False)
            step(NT + 1, 1, scores=False, probs=False)

            act.wait_ge(tw_in, 16 * 11)
            act.activation(tg[:, 1:2], tg[:, 0:1], ACT.Tanh).then_inc(tanh_ok, 1)
            n = [0]

            def done(ins):
                n[0] += 1
                ins.then_inc(ta, 1)

            act.wait_ge(tv, V_VAR1)
            done(act.activation(sd[:], mv[:, :, 1], ACT.Sqrt))
            act.wait_ge(tp, PT_LN1)
            done(act.activation(lnT[:, 0, :], trp[0][:], ACT.Copy))
            for m in range(MT):
                act.wait_ge(tp, PT_V + m + 1)
                done(act.activation(v_sb[:, m, :], scp[:, m, :], ACT.Copy))
            act.wait_ge(tv, V_KSUB)
            done(act.activation(ke[:], ke[:], ACT.Exp))
            act.wait_ge(tv, V_QSUB)
            done(act.activation(qe[:], qe[:], ACT.Exp))
            for m in range(0, MT, 2):
                act.wait_ge(tp, PT_KT + m + 1)
                done(act.activation(kn[:, m, :], scp[:, m, :], ACT.Copy))
            for m in range(0, HP, 2):
                act.wait_ge(tp, PT_QT + m + 1)
                done(act.activation(lqT[:, m, :], [trp[0], trp[1], up, wp][m][:], ACT.Copy))
            for t in range(HP):
                act.wait_ge(tp, PT_OT)
                done(act.activation(lo_T[:, t, :], scp[:, t, :], ACT.Copy))
            act.wait_ge(tv, V_VAR2)
            done(act.activation(sd[:], mv[:, :, 1], ACT.Sqrt))
            act.wait_ge(tp, PT_LN2)
            for dt in range(DT):
                done(act.activation(lnT_hi[:, dt, :], trp[dt][:], ACT.Copy))
            act.wait_ge(tv, V_TDIFF)
            done(act.activation(texp[:], tdiff[:], ACT.Exp))

            def expert(i, s):
                for f in range(FT):
                    k = (i * 2 + s) * FT + f
                    act.wait_ge(h_ok, k + 1)
                    wait(act, hl_ok, k - 1)
                    act.activation(h_f[:, f % 2, :], hbank(f), ACT.Relu,
                                   bias=b1_ap(i, s, f)).then_inc(hf_ok, 1)
            act.wait_ge(small_in, 64)
            expert(0, 0)
            expert(0, 1)
            with act.Fori(1, NE // 2) as i:
                expert(i, 0)
                expert(i, 1)

        @block.vector
        def _(dve):
            steps = [0]

            def link(ins):
                steps[0] += 1
                ins.then_inc(dve_step, 1)
                dve.wait_ge(dve_step, steps[0])

            def norm_stats(src, m):
                link(dve.bn_stats(stats[:, m, :], src))
                link(dve.bn_aggr(mv[:, m, :], stats[:, m, :]))

            for r in range(2):
                for m in range(MT):
                    if r == 0:
                        dve.wait_ge(x_in, 16 * MT)
                    norm_stats(x_sb[:, m, :] if r == 0 else xn[:, m, :], m)
                dve.tensor_scalar(mv[:, :, 1], mv[:, :, 1], EPS, None, ALU.add).then_inc(var_ok, 1)
                dve.wait_ge(sd_ok, r + 1)
                link(dve.reciprocal(rstd[:], sd[:]))
                for m in range(MT):
                    src = x_sb[:, m, :] if r == 0 else xn[:, m, :]
                    link(dve.tensor_scalar(xn[:, m, :], src, mv[:, m, 0:1], rstd[:, m:m + 1],
                                           ALU.subtract, ALU.mult))
            dve.wait_ge(small_in, 32)
            for m in range(MT):
                link(dve.tensor_tensor(xn[:, m, :], xn[:, m, :], gamma_b[:], ALU.mult))
                dve.tensor_tensor(xn[:, m, :], xn[:, m, :], beta_b[:], ALU.add).then_inc(xn_ok, 1)
            for t in range(TPB):
                if t >= 2:
                    dve.wait_ge(qk_out[t % 2], 16 * (t // 2))
                for dt in range(DT):
                    dve.wait_ge(pro_k, DT * t + dt + 1)
                    dve.tensor_copy(stage[:, t % 2, :, dt * P + Q:(dt + 1) * P],
                                    scp[:, 2 * dt + 1, :].rearrange("p (b q) -> p b q", q=Q)).then_inc(pro_kc_dve, 1)

            def take_u(m, slot):
                dve.wait_ge(ub_ok, m + 1)
                wait(dve, ut_ok, m)
                dve.scalar_tensor_tensor(out=u_sb[:], in0=up[:, 0:D], scalar=rsum[:, slot:slot + 1], in1=u_b[:],
                                         op0=ALU.mult, op1=ALU.add).then_inc(u_ok, 1)

            def take_lo(m, g):
                j0, j1 = 4 * g, min(4 * g + 4, SJ)
                dve.wait_ge(hi_ok, m * SG + g + 1)
                if j1 < SJ:
                    dve.tensor_tensor(pt_lo[:, j0:j1, :], trp[g % 2][:].rearrange("p (j q) -> p j q", q=P),
                                      pt_hi[:, j0:j1, :].bitcast(F32), ALU.subtract).then_inc(lo_ok, 1)
                else:
                    dve.tensor_tensor(pt_lo[0:SL, j0, :], trp[g % 2][0:SL, 0:P],
                                      pt_hi[0:SL, j0, :].bitcast(F32), ALU.subtract).then_inc(lo_ok, 1)

            def row_sum(m, slot):
                dve.wait_ge(exp_ok, (m + 1) * 2)
                dve.tensor_tensor(tsum[:, slot:slot + 1], esum[:, slot, 0:1], esum[:, slot, 1:2],
                                  ALU.add).then_inc(tsum_ok, 1)
                dve.wait_ge(tsum_ok, m + 1)
                dve.reciprocal(rsum[:, slot:slot + 1], tsum[:, slot:slot + 1]).then_inc(rsum_ok, 1)

            def take_o(m, t, tok0):
                dve.wait_ge(wv_ok, m + 1)
                dve.tensor_copy(oT[0:Q, t, tok0], wp[0:Q, 2 * P:2 * P + Q])
                dve.tensor_copy(oT[Q:P, t, tok0], wp[Q:P, 2 * P + Q:3 * P]).then_inc(o_ok, 1)

            def step(n, u, tok, first=False, scores=True, probs=True):
                lag1 = probs and not (first and u < 1)
                lag2 = not (first and u < 2)
                if lag2:
                    take_u(n - 2, u % 2)
                if lag1:
                    take_lo(n - 1, 0)
                    row_sum(n - 1, (u + 1) % 2)
                    take_lo(n - 1, 1)
                    take_lo(n - 1, 2)
                if scores:
                    dve.wait_ge(scores_ok, n * 2 + 1)
                    dve.tensor_reduce(mx2[:, u % 2, 0:1], scp[:, 0:3, 0:CW], AX.XY, ALU.max).then_inc(pmax_ok, 1)
                if lag1:
                    take_lo(n - 1, 3)
                if lag2:
                    take_o(n - 2, (u - 2) % TPB, tok((u - 2) // TPB))
                if scores:
                    dve.wait_ge(scores_ok, n * 2 + 2)
                    dve.tensor_reduce(mx2[:, u % 2, 1:2], scp[:, 3, 0:CREAL[3]], AX.X, ALU.max).then_inc(pmax_ok, 1)
                    dve.wait_ge(pmax_ok, n * 2 + 2)
                    dve.tensor_reduce(nmax[:, u % 2:u % 2 + 1], mx2[:, u % 2, :], AX.X, ALU.max,
                                      negate=True).then_inc(nmax_ok, 1)

            for u in range(PAIR):
                step(u, u, lambda b: slice(b * Q, (b + 1) * Q), first=True)
            with dve.Fori(1, NT // PAIR) as i:
                for u in range(PAIR):
                    step(i * PAIR + u, u, lambda b: bass.ds(i * (2 * Q) + b * Q, Q))
            step(NT, 0, lambda b: slice((B + b) * Q, (B + b + 1) * Q), scores=False)
            step(NT + 1, 1, lambda b: slice((B + b) * Q, (B + b + 1) * Q), scores=False, probs=False)

            n = [0]

            def done(ins):
                n[0] += 1
                ins.then_inc(tv, 1)

            def then(ins):
                done(ins)
                dve.wait_ge(tv, n[0])

            def at(want, name):
                assert n[0] == want, (name, n[0], want)

            def layer_norm(src, act_count):
                for m in range(MT):
                    then(dve.bn_stats(stats[:, m, :], src[:, m, :]))
                    then(dve.bn_aggr(mv[:, m, :], stats[:, m, :]))
                then(dve.tensor_scalar(mv[:, :, 1], mv[:, :, 1], EPS, None, ALU.add))
                dve.wait_ge(ta, act_count)
                then(dve.reciprocal(rstd[:], sd[:]))
                for m in range(MT):
                    done(dve.tensor_scalar(ln_out[:, m, :], src[:, m, :], mv[:, m, 0:1], rstd[:, m:m + 1],
                                           ALU.subtract, ALU.mult))

            dve.wait_ge(tw_in, 16 * 11)
            dve.wait_ge(tanh_ok, 1)
            for m in range(MT):
                dve.wait_ge(tp, m + 1)
                then(dve.tensor_tensor(xa[:, m, :], scp[:, m, 0:D], bout_b[:], ALU.add))
                then(dve.scalar_tensor_tensor(out=x1[:, m, :], in0=xa[:, m, :], scalar=tg[:, 1:2], in1=x_sb[:, m, :],
                                              op0=ALU.mult, op1=ALU.add))
            layer_norm(x1, 1)
            at(V_LN1, "V_LN1")
            dve.wait_ge(tp, PT_LN1)
            done(dve.tensor_copy(lnT[:, 1, :], trp[1][:]))
            at(V_LNT1, "V_LNT1")
            done(dve.memset(cbd[:].rearrange("p b t e -> p (b t e)"), 0.0))
            then(dve.memset(bmask[:], 0.0))
            done(dve.memset(bmask[0:Q, 0:Q], 1.0))
            done(dve.memset(bmask[Q:P, Q:P], 1.0))
            for t in range(HP):
                dve.wait_ge(tp, PT_K + t + 1)
                ps = scp[:, t, :].rearrange("p (b n) -> p b n", n=Q)
                then(dve.tensor_reduce(lmax[:, 0, t, :], ps, AX.X, ALU.max))
                done(dve.tensor_tensor(ke[:, t, :].rearrange("p (b n) -> p b n", n=Q), ps,
                                       lmax[:, 0, t, :].unsqueeze(2).broadcast_to((P, 8, Q)), ALU.subtract))
            at(V_KSUB, "V_KSUB")
            for m in range(MT):
                dve.wait_ge(tp, PT_Q + m + 1)
                ps = [trp[0], trp[1], up, wp][m][:].rearrange("p (b n) -> p b n", n=LD)
                then(dve.tensor_reduce(lmax[:, 1, m, :], ps, AX.X, ALU.max))
                done(dve.tensor_tensor(qe[:, m, :].rearrange("p (b n) -> p b n", n=LD), ps,
                                       lmax[:, 1, m, :].unsqueeze(2).broadcast_to((P, 8, LD)), ALU.subtract))
            at(V_QSUB, "V_QSUB")
            for w, (buf, cnt) in enumerate(((ke, 7), (qe, 8))):
                dve.wait_ge(ta, cnt)
                v3 = buf[:].rearrange("p t (b n) -> p (t b) n", n=Q)
                r2 = lrec[:, w, :, :].rearrange("p t b -> p (t b)")
                then(dve.tensor_reduce(lsum[:, w, :, :].rearrange("p t b -> p (t b)"), v3, AX.X, ALU.add))
                then(dve.reciprocal(r2, lsum[:, w, :, :].rearrange("p t b -> p (t b)")))
                if w == 1:
                    then(dve.tensor_scalar(r2, r2, float(LD) ** -0.5, None, ALU.mult))
                done(dve.tensor_tensor(v3, v3, r2.unsqueeze(2).broadcast_to((P, 32, Q)), ALU.mult))
                at((V_KN, V_QN)[w], "V_KN/V_QN")
            for m in range(1, MT, 2):
                dve.wait_ge(tp, PT_KT + m + 1)
                done(dve.tensor_copy(kn[:, m, :], scp[:, m, :]))
            for m in range(1, HP, 2):
                dve.wait_ge(tp, PT_QT + m + 1)
                done(dve.tensor_copy(lqT[:, m, :], [trp[0], trp[1], up, wp][m][:]))
            at(V_QTC, "V_QTC")
            for b in range(B):
                dve.wait_ge(tp, PT_CTX + b + 1)
                done(dve.tensor_tensor(cbd[:, b, :, :], [trp[0], trp[1], up, wp][b % 4][:].rearrange("p (t e) -> p t e", e=P),
                                       bmask[:].unsqueeze(1).broadcast_to((P, HP, P)), ALU.mult))
            at(V_CBD, "V_CBD")
            for m in range(MT):
                dve.wait_ge(tp, PT_Y + m + 1)
                then(dve.tensor_tensor(xa[:, m, :], scp[:, m, 0:D], bo_b[:], ALU.add))
                then(dve.tensor_tensor(xa[:, m, :], xa[:, m, :], x1[:, m, :], ALU.add))
            layer_norm(xa, 17)
            at(V_LN2, "V_LN2")
            dve.wait_ge(tp, PT_LN2)
            dve.wait_ge(ta, 19)
            for dt in range(DT):
                done(dve.tensor_tensor(lnT_lo[:, dt, :], trp[dt][:], lnT_hi[:, dt, :].bitcast(F32), ALU.subtract))
            for dt in range(DT):
                done(dve.tensor_copy(lnT[:, dt, :], trp[dt][:]))
            at(V_LNT2, "V_LNT2")
            dve.wait_ge(tp, PT_R)
            for m in range(MT):
                then(dve.tensor_tensor(logit[:, m, :], up[:, m * NE:(m + 1) * NE], br_b[:], ALU.add))
                then(dve.max(top[:, m, :], logit[:, m, :]))
                then(dve.max_index(topi[:, m, :], top[:, m, :], logit[:, m, :]))
            done(dve.tensor_copy(topf[:], topi[:, :, 0:2]))
            done(dve.tensor_tensor(tdiff[:], top[:, :, 1], top[:, :, 0], ALU.subtract))
            at(V_TDIFF, "V_TDIFF")
            dve.wait_ge(tv, n[0])
            dve.wait_ge(ta, 20)
            then(dve.tensor_scalar(sd[:], texp[:], 1.0, None, ALU.add))
            then(dve.reciprocal(tw[:, :, 0], sd[:]))
            then(dve.tensor_tensor(tw[:, :, 1], tw[:, :, 0], texp[:], ALU.mult))
            dve.wait_ge(tq, 1)
            for m in range(MT):
                then(dve.tensor_scalar(gw[:, m, :], eidx[:], topf[:, m, 0:1], tw[:, m, 0:1], ALU.is_equal, ALU.mult))
                then(dve.tensor_scalar(sel[:, m, :], eidx[:], topf[:, m, 1:2], tw[:, m, 1:2], ALU.is_equal, ALU.mult))
                then(dve.tensor_tensor(gw[:, m, :], gw[:, m, :], sel[:, m, :], ALU.add))
            at(V_GW, "V_GW")
            dve.wait_ge(tp, PT_GT)
            done(dve.tensor_copy(gwT[:], up[0:NE, :]))
            at(V_GWT, "V_GWT")
            for m in range(MT):
                dve.wait_ge(tp, PT_B2)
                then(dve.tensor_tensor(xa[:, m, :], xa[:, m, :], scp[:, m, 0:D], ALU.add))
            at(V_B2, "V_B2")

            def gate_ap(i, s, m):
                if isinstance(i, int):
                    return gw[:, m, i * 2 + s:i * 2 + s + 1]
                return gw[:].rearrange("p m e -> p (m e)")[:, bass.ds(i * 2 + (m * NE + s), 1)]

            def expert(i, s):
                for f in range(FT):
                    k = (i * 2 + s) * FT + f
                    dve.wait_ge(hf_ok, k + 1)
                    wait(dve, y_ok, k - (FT - 1))
                    dve.tensor_copy(h_hi[:, f, :], h_f[:, f % 2, :]).then_inc(hh_ok, 1)
                    dve.wait_ge(hh_ok, k + 1)
                    dve.tensor_tensor(h_lo[:, f, :], h_f[:, f % 2, :], h_hi[:, f, :].bitcast(F32),
                                      ALU.subtract).then_inc(hl_ok, 1)
                for m in range(MT):
                    k = (i * 2 + s) * MT + m
                    dve.wait_ge(y_ok, (i * 2 + s + 1) * FT)
                    dve.scalar_tensor_tensor(out=xa[:, m, :], in0=scp[:, m, 0:D], scalar=gate_ap(i, s, m),
                                             in1=xa[:, m, :], op0=ALU.mult, op1=ALU.add).then_inc(y_stage, 1)
                    dve.wait_ge(y_stage, k + 1)
                    dve.scalar_tensor_tensor(out=xa[:, m, :], in0=scp[:, m, D:2 * D], scalar=gate_ap(i, s, m),
                                             in1=xa[:, m, :], op0=ALU.mult, op1=ALU.add).then_inc(yc_ok, 1)

            expert(0, 0)
            expert(0, 1)
            with dve.Fori(1, NE // 2) as i:
                expert(i, 0)
                expert(i, 1)

        @block.tensor
        def _(pe):
            pe.wait_ge(ident_ok, 1)
            pe.wait_ge(xn_ok, MT)
            for dt in range(DT):
                for m in range(MT):
                    ins = pe.transpose(trp[dt][:, m * P:(m + 1) * P], xn[:, m, dt * P:(dt + 1) * P], ident[:])
                ins.then_inc(pro_tr, 1)
            pe.wait_ge(pw_in, 32)
            pe.wait_ge(pro_trc, DT)
            for t in range(TPB):
                if t >= NC:
                    pe.wait_ge(pro_qc, t - NC + 1)
                for dt in range(DT):
                    ins = pe.matmul(scp[:, t % NC, :], wq_sb[:, dt, t * P:(t + 1) * P], xnT[:, dt, :],
                                    start=dt == 0, stop=dt == DT - 1)
                ins.then_inc(pro_q, 1)
            pe.wait_ge(pro_qc, TPB)
            for t in range(TPB):
                for dt in range(DT):
                    if t >= 1:
                        pe.wait_ge(pro_kc_act, DT * (t - 1) + dt + 1)
                        pe.wait_ge(pro_kc_dve, DT * (t - 1) + dt + 1)
                    for par in range(2):
                        rows = slice(par * Q, (par + 1) * Q)
                        ins = pe.matmul(scp[:, 2 * dt + par, :], wkt_sb[rows, t, dt * P:(dt + 1) * P], qT[rows, t, :],
                                        start=True, stop=True)
                    ins.then_inc(pro_k, 1)

            def scores(n, u, c):
                slot, par = u % 2, u // TPB
                if c == 0:
                    pe.wait_ge(qk_ready, n + 1)
                    wait(pe, exp_ok, n * 2 - 1)
                if c == 3:
                    wait(pe, exp_ok, n * 2)
                cs = slice(c * CW, c * CW + CWID[c])
                k = 0
                for dt in range(DT):
                    ds_ = slice(dt * P, (dt + 1) * P)
                    for w, v in ((qk_hi, ct_hi), (qk_hi, ct_lo), (qk_lo, ct_hi)):
                        ins = pe.matmul(scp[:, c, 0:CWID[c]], w[:, slot, ds_], v[:, par, dt, cs],
                                        start=k == 0, stop=k == 5)
                        k += 1
                if c >= 2:
                    ins.then_inc(scores_ok, 1)

            def transposes(m, g):
                j0, j1 = 4 * g, min(4 * g + 4, SJ)
                if g % 2 == 0:
                    pe.wait_ge(exp_ok, m * 2 + 1 + g // 2)
                G = m * SG + g
                wait(pe, lo_ok, G - 1)
                for j in range(j0, j1):
                    r = P if j < SJ - 1 else SL
                    ins = pe.transpose(trp[g % 2][0:r, (j - j0) * P:(j - j0 + 1) * P], prob[:, j * P:j * P + r], ident[:])
                ins.then_inc(tr_ok, 1)

            def times_context(m, par):
                wait(pe, u_ok, m)
                for j in range(SJ):
                    r = P if j < SJ - 1 else SL
                    if j % 4 == 0:
                        pe.wait_ge(lo_ok, m * SG + j // 4 + 1)
                    pe.matmul(up[:, 0:2 * D], pt_hi[0:r, j, :], cn[0:r, par, j, :], start=j == 0, stop=False)
                    ins = pe.matmul(up[:, 0:D], pt_lo[0:r, j, :], cn[0:r, par, j, 0:D], start=False, stop=j == SJ - 1)
                ins.then_inc(pv_ok, 1)

            def transpose_u(m):
                pe.wait_ge(u_ok, m + 1)
                wait(pe, o_ok, m)
                for dt in range(DT):
                    ins = pe.transpose(wp[:, dt * P:(dt + 1) * P], u_sb[:, dt * P:(dt + 1) * P], ident[:])
                ins.then_inc(ut_ok, 1)

            def times_wv(m, t):
                pe.wait_ge(utc_ok, m + 1)
                for dt in range(DT):
                    ins = pe.matmul(wp[:, 2 * P:3 * P], wv_sb[:, dt, t * P:(t + 1) * P], ut_sb[:, dt, :],
                                    start=dt == 0, stop=dt == DT - 1)
                ins.then_inc(wv_ok, 1)

            def step(n, u, batch, first=False, do_scores=True, probs=True):
                lag1 = probs and not (first and u < 1)
                lag2 = not (first and u < 2)
                if do_scores and u % TPB == 0:
                    pe.wait_ge(ct_ready, (batch + u // TPB + 1) * NCT)
                for g in range(4):
                    if do_scores:
                        scores(n, u, g)
                    if g == 3 and lag2:
                        times_wv(n - 2, (u - 2) % TPB)
                    if lag1:
                        transposes(n - 1, g)
                    if g == 1 and lag2:
                        transpose_u(n - 2)
                if lag1:
                    if u % TPB == 1:
                        pe.wait_ge(cn_ready, (batch + u // TPB + 1) * NCN)
                    times_context(n - 1, ((u - 1) // TPB) % 2)

            pe.wait_ge(tw_in, 16 * 11)
            for u in range(PAIR):
                step(u, u, 0, first=True)
            with pe.Fori(1, NT // PAIR) as i:
                for u in range(PAIR):
                    step(i * PAIR + u, u, i * 2)
            step(NT, 0, B, do_scores=False)
            step(NT + 1, 1, B, do_scores=False, probs=False)

            n = [0]

            def done(ins):
                n[0] += 1
                ins.then_inc(tp, 1)

            def at(want, name):
                assert n[0] == want, (name, n[0], want)

            quad = [trp[0], trp[1], up, wp]
            pe.wait_ge(o_ok, NT)
            pe.wait_ge(exp_ok, 2 * NT)
            for m in range(MT):
                for t in range(TPB):
                    ins = pe.matmul(scp[:, m, 0:D], oT[:, t, m * P:(m + 1) * P], wout_sb[:, t, :],
                                    start=t == 0, stop=t == TPB - 1)
                done(ins)
            at(OUT_PE, "OUT_PE")
            pe.wait_ge(tv, V_LN1)
            for dt in range(DT):
                for m in range(MT):
                    ins = pe.transpose(trp[dt][:, m * P:(m + 1) * P], ln_out[:, m, dt * P:(dt + 1) * P], ident[:])
            done(ins)
            at(PT_LN1, "PT_LN1")
            pe.wait_ge(ta, 2)
            pe.wait_ge(tv, V_LNT1)
            for t in range(HP):
                for dt in range(DT):
                    ins = pe.matmul(scp[:, t, :], lw_sb[:, 1, dt, t * P:(t + 1) * P], lnT[:, dt, :],
                                    start=dt == 0, stop=dt == DT - 1)
                done(ins)
            at(PT_Q, "PT_Q")
            for m in range(MT):
                for dt in range(DT):
                    ins = pe.matmul(quad[m][:], lnT[:, dt, m * P:(m + 1) * P], lw_sb[:, 0, dt, :],
                                    start=dt == 0, stop=dt == DT - 1)
                done(ins)
            at(PT_V, "PT_V")
            pe.wait_ge(tv, V_KSUB)
            for m in range(MT):
                for dt in range(DT):
                    ins = pe.matmul(scp[:, m, :], lnT[:, dt, m * P:(m + 1) * P], lw_sb[:, 2, dt, :],
                                    start=dt == 0, stop=dt == DT - 1)
                done(ins)
            at(PT_KT, "PT_KT")
            pe.wait_ge(ta, 6)
            pe.wait_ge(tv, V_KN)
            for m in range(MT):
                for t in range(HP):
                    ins = pe.transpose(scp[:, m, t * P:(t + 1) * P], ke[:, t, m * P:(m + 1) * P], ident[:])
                done(ins)
            at(PT_QT, "PT_QT")
            pe.wait_ge(tv, V_QN)
            for t in range(HP):
                for m in range(MT):
                    ins = pe.transpose(quad[t][:, m * P:(m + 1) * P], qe[:, m, t * P:(t + 1) * P], ident[:])
                done(ins)
            at(PT_CTX, "PT_CTX")
            pe.wait_ge(ta, 12)
            pe.wait_ge(tv, V_QTC)
            for b in range(B):
                if b >= 4:
                    pe.wait_ge(tv, V_QTC + b - 3)
                rows = slice((b % 2) * Q, (b % 2 + 1) * Q)
                for t in range(HP):
                    ins = pe.matmul(quad[b % 4][:, t * P:(t + 1) * P], kn[rows, b // 2, t * P:(t + 1) * P],
                                    v_sb[rows, b // 2, t * P:(t + 1) * P], start=True, stop=True)
                done(ins)
            at(PT_CTX + B, "ctx")
            pe.wait_ge(tv, V_CBD)
            for t in range(HP):
                for b in range(B):
                    ins = pe.matmul(scp[:, t, b * Q:(b + 1) * Q], cbd[:, b, t, :], lqT[:, t, b * Q:(b + 1) * Q],
                                    start=True, stop=True)
            done(ins)
            at(PT_OT, "PT_OT")
            pe.wait_ge(ta, 16)
            for m in range(MT):
                for t in range(HP):
                    ins = pe.matmul(scp[:, m, 0:D], lo_T[:, t, m * P:(m + 1) * P], wo_sb[:, t, :],
                                    start=t == 0, stop=t == HP - 1)
                done(ins)
            at(LIN_PE, "LIN_PE")
            pe.wait_ge(tv, V_LN2)
            for dt in range(DT):
                for m in range(MT):
                    ins = pe.transpose(trp[dt][:, m * P:(m + 1) * P], ln_out[:, m, dt * P:(dt + 1) * P], ident[:])
            done(ins)
            at(PT_LN2, "PT_LN2")
            pe.wait_ge(tv, V_LNT2)
            for m in range(MT):
                for dt in range(DT):
                    ins = pe.matmul(up[:, m * NE:(m + 1) * NE], lnT[:, dt, m * P:(m + 1) * P], wr_sb[:, dt, :],
                                    start=dt == 0, stop=dt == DT - 1)
            done(ins)
            at(PT_R, "PT_R")
            pe.wait_ge(tv, V_GW)
            for m in range(MT):
                ins = pe.transpose(up[0:NE, m * P:(m + 1) * P], gw[:, m, :], ident[:])
            done(ins)
            at(PT_GT, "PT_GT")
            pe.wait_ge(tv, V_GWT)
            pe.wait_ge(small_in, 64)
            for m in range(MT):
                ins = pe.matmul(scp[:, m, 0:D], gwT[:, m * P:(m + 1) * P], b2_sb[:], start=True, stop=True)
            done(ins)
            at(PT_B2, "PT_B2")
            pe.wait_ge(tv, V_B2)

            def expert(i, s):
                e = i * 2 + s
                for f in range(FT):
                    k = e * FT + f
                    if f == 0:
                        pe.wait_ge(w_ready, (e + 1) * 3)
                    wait(pe, hf_ok, k - 3)
                    c = 0
                    for dt in range(DT):
                        for w, v in ((w1_hi, lnT_hi), (w1_hi, lnT_lo), (w1_lo, lnT_hi)):
                            ins = pe.matmul(hbank(f), w[:, s, dt, f * P:(f + 1) * P], v[:, dt, :],
                                            start=c == 0, stop=c == 5)
                            c += 1
                    ins.then_inc(h_ok, 1)
                for f in range(FT):
                    pe.wait_ge(hl_ok, e * FT + f + 1)
                    for m in range(MT):
                        if f == 0:
                            wait(pe, yc_ok, e * MT + m - (MT - 1))
                        ms = slice(m * P, (m + 1) * P)
                        pe.matmul(scp[:, m, :], h_hi[:, f, ms], w2_sp[:, s, f, :], start=f == 0, stop=False)
                        ins = pe.matmul(scp[:, m, 0:D], h_lo[:, f, ms], w2_sp[:, s, f, 0:D],
                                        start=False, stop=f == FT - 1)
                    ins.then_inc(y_ok, 1)

            expert(0, 0)
            expert(0, 1)
            with pe.Fori(1, NE // 2) as i:
                expert(i, 0)
                expert(i, 1)


OUT_PE = MT
PT_LN1 = OUT_PE + 1
PT_K = PT_LN1
PT_Q = PT_K + HP
PT_V = PT_Q + MT
PT_KT = PT_V + MT
PT_QT = PT_KT + MT
PT_CTX = PT_QT + HP
PT_OT = PT_CTX + B + 1
PT_Y = PT_OT
LIN_PE = PT_Y + MT
PT_LN2 = LIN_PE + 1
PT_R = PT_LN2 + 1
PT_GT = PT_R + 1
PT_B2 = PT_GT + 1
V_X1 = 2 * MT
V_VAR1 = V_X1 + 2 * MT + 1
V_LN1 = V_VAR1 + 1 + MT
V_LNT1 = V_LN1 + 1
V_KSUB = V_LNT1 + 4 + 2 * HP
V_QSUB = V_KSUB + 2 * MT
V_KN = V_QSUB + 3
V_QN = V_KN + 4
V_QTC = V_QN + MT // 2 + HP // 2
V_CBD = V_QTC + B
V_X2 = V_CBD + 2 * MT
LIN_DVE = V_CBD
V_VAR2 = V_X2 + 2 * MT + 1
V_LN2 = V_VAR2 + 1 + MT
V_LNT2 = V_LN2 + 2 * DT
V_TDIFF = V_LNT2 + 3 * MT + 2
V_GW = V_TDIFF + 3 + 3 * MT
V_GWT = V_GW + 1
V_B2 = V_GWT + MT


def kernel(**inputs):
    import numpy as np
    import concourse.bacc as bacc
    from concourse.bass_utils import run_bass_kernel_spmd

    a = {k: np.asarray(v) for k, v in inputs.items()}
    inner = H * DH
    w_kv = a["L0_xattn_w_kv"]
    arrays = {
        "x": a["x"].reshape(TOK, D),
        "ctx_n": a["ctx_1024"],
        "ctx_t": a["ctx_1024"].transpose(0, 2, 1),
        "gamma": a["L0_xattn_ln_gamma"],
        "beta": a["L0_xattn_ln_beta"],
        "w_q": a["L0_xattn_w_q"],
        "w_kt": w_kv[:, :inner].T,
        "w_v": w_kv[:, inner:],
        "w_out": a["L0_xattn_w_out"],
        "b_out": a["L0_xattn_b_out"],
        "gate": a["L0_xattn_gate"],
        "Wq": a["L0_attn_Wq"], "Wk": a["L0_attn_Wk"], "Wv": a["L0_attn_Wv"], "Wo": a["L0_attn_Wo"],
        "bo": a["L0_attn_bo"],
        "W_router": a["L0_ffn_W_router"], "b_router": a["L0_ffn_b_router"],
        "W1": a["L0_ffn_W1"],
        "b1": a["L0_ffn_b1"].reshape(NE, FT, P).transpose(2, 0, 1),
        "W2": a["L0_ffn_W2"],
        "b2": a["L0_ffn_b2"],
    }
    arrays = {k: np.ascontiguousarray(v) for k, v in arrays.items()}
    nc = bacc.Bacc("TRN2", target_bir_lowering=False, num_devices=1)
    args = [nc.dram_tensor(k, v.shape, mybir.dt.from_np(v.dtype), kind="ExternalInput").ap()
            for k, v in arrays.items()]
    out = nc.dram_tensor("out", (TOK, D), F32, kind="ExternalOutput").ap()
    build(nc, *args, out)
    r = run_bass_kernel_spmd(nc, [arrays], core_ids=[0])
    return r.results[0]["out"].reshape(B, Q, D)
```

```python
from contextlib import ExitStack

import concourse.bass as bass
from concourse import mybir

F32 = mybir.dt.float32
F32R = mybir.dt.float32r
U32 = mybir.dt.uint32
ALU = mybir.AluOpType
ACT = mybir.ActivationFunctionType
AX = mybir.AxisListType

P = 128
B, Q, D = 8, 64, 256
S = 1601
SP = S + 1
H, DH = 16, 64
TOK = B * Q
MT = TOK // P
DT = D // P
TPB = H * Q // P
GT = 4
GW = GT * P
NG = B * TPB // GT
GPB = NG // B
SJ = (S + P - 1) // P
SL = S - (SJ - 1) * P
NSLOT = NG * SJ
CNW = 2 * D + 2
L_SUB, L_LO, L_PV = SJ + 4, SJ + 5, SJ + 6
PASS = 4 * SJ
NPASS = NSLOT // PASS
V_U, V_UT, V_UTC, V_WV, V_O = 6, 6, 7, 8, 9
RR = 4
PR = 4
LH, LD = 8, 64
HID = LH * LD
HP = HID // P
NE, FF = 8, 1024
FT = FF // P
EPS = 1e-5

UNIT_LEAD = 6


def slot_jobs(k):
    g, j = k // SJ, k % SJ
    jobs = []
    if SJ <= k + UNIT_LEAD < 2 * SJ * B:
        jobs.append(("ctx", k + UNIT_LEAD))
    if j in (1, 4, 7, 10) and g + 1 < NG:
        jobs.append(("qk", g + 1, j // 3))
    return jobs


FIRST_JOBS = [("ctx", w) for w in range(SJ)] + [("qk", 0, t) for t in range(GT)]
JOBS = FIRST_JOBS + [job for k in range(NSLOT) for job in slot_jobs(k)]
JOB_NO = {job: n for n, job in enumerate(JOBS)}


def shift(job, passes):
    if job[0] == "ctx":
        return ("ctx", job[1] + passes * PASS)
    return ("qk", job[1] + passes * (PASS // SJ), job[2])


def linear(i, f):
    if isinstance(i, int):
        return f(i)
    return i * (f(2) - f(1)) + f(1)


def build(nc, x, ctx_n, ctx_t, gamma, beta, w_q, w_kt, w_v, w_out, b_out, gate, Wq, Wk, Wv, Wo, bo,
          W_router, b_router, W1, b1, W2, b2, out):
    with ExitStack() as es:
        def sb(name, shape, dt=F32):
            return es.enter_context(nc.sbuf_tensor(name, shape, dt))

        def sem(name):
            return es.enter_context(nc.semaphore(name))

        qk_dram = nc.dram_tensor("qk_scratch", (B * TPB, P, DT * P), F32, kind="Internal").ap()

        x_sb = sb("x_sb", [P, MT, D])
        ident = sb("ident", [P, P])
        gamma_b = sb("gamma_b", [P, D])
        beta_b = sb("beta_b", [P, D])
        bout_b = sb("bout_b", [P, D])
        bo_b = sb("bo_b", [P, D])
        tg = sb("tg", [P, 2])
        zero = sb("zero", [P, 1])
        stats = sb("stats", [P, MT, 6])
        mv = sb("mv", [P, MT, 2])
        sd = sb("sd", [P, MT])
        rstd = sb("rstd", [P, MT])
        wv_sb = sb("wv_sb", [P, DT, H * DH])
        wout_sb = sb("wout_sb", [P, TPB, D])
        oT = sb("oT", [P, TPB, TOK])
        stage = oT[:].rearrange("p t (a f) -> p (t a) f", f=2 * P).rearrange("p (s b) f -> p s b f", s=2)
        wo_sb = sb("wo_sb", [P, HP, D])
        wr_sb = sb("wr_sb", [P, DT, NE])
        br_b = sb("br_b", [P, NE])
        loop_scope = ExitStack()

        def lsb(name, shape, dt=F32):
            return loop_scope.enter_context(nc.sbuf_tensor(name, shape, dt))

        ct_hi = lsb("ct_hi", [P, DT, S], F32R)
        ct_lo = lsb("ct_lo", [P, DT, S], F32R)
        cn = lsb("cn", [P, SJ, CNW], F32R)
        raw = lsb("raw", [P, RR, DT, P])
        qk_hi = lsb("qk_hi", [P, 2, DT, GW], F32R)
        qk_lo = lsb("qk_lo", [P, 2, DT, GW], F32R)
        mtouch = lsb("mtouch", [P, 1])
        rsum = lsb("rsum", [P, GT])
        u_sb = lsb("u_sb", [P, GT, D])
        ut_sb = lsb("ut_sb", [P, GT, DT, P])
        pro_scope = ExitStack()

        def psb(name, shape):
            return pro_scope.enter_context(nc.sbuf_tensor(name, shape, F32))

        wq_sb = psb("wq_sb", [P, DT, H * DH])
        wkt_sb = psb("wkt_sb", [P, TPB, D])
        qT = psb("qT", [P, TPB, TOK])
        xn = psb("xn", [P, MT, D])
        xnT = psb("xnT", [P, DT, TOK])
        pro_scope.close()
        st = lsb("st", [P, 2, SJ, GW])
        cmax = lsb("cmax", [P, 2, GW])
        mbc = lsb("mbc", [P, 2, GW])
        pt_hi = lsb("pt_hi", [P, PR, GW], F32R)
        pt_lo = lsb("pt_lo", [P, PR, GW], F32R)
        loop_scope.close()
        tail = ExitStack()

        def tsb(name, shape, dt=F32):
            return tail.enter_context(nc.sbuf_tensor(name, shape, dt))

        lw_sb = tsb("lw_sb", [P, 3, DT, HID])
        w1_hi = tsb("w1_hi", [P, 2, DT, FF], F32R)
        w1_lo = tsb("w1_lo", [P, 2, DT, FF], F32R)
        w2_sp = tsb("w2_sp", [P, 2, FT, 2 * D], F32R)
        x1 = tsb("x1", [P, MT, D])
        xa = tsb("xa", [P, MT, D])
        ln_out = stage[:, 1, B // 2:B, :]
        lnT = tsb("lnT", [P, DT, TOK])
        lnT_hi = tsb("lnT_hi", [P, DT, TOK], F32R)
        lnT_lo = tsb("lnT_lo", [P, DT, TOK], F32R)
        lin = ExitStack()

        def nsb(name, shape, dt=F32):
            return lin.enter_context(nc.sbuf_tensor(name, shape, dt))

        ke = nsb("ke", [P, HP, TOK])
        kn = nsb("kn", [P, MT, HID])
        qe = nsb("qe", [P, MT, HID])
        lqT = nsb("lqT", [P, HP, TOK])
        v_sb = nsb("v_sb", [P, MT, HID])
        cbd = nsb("cbd", [P, B, HP, P])
        lo_T = stage[:, 0, :, :].rearrange("p (t b) f -> p t (b f)", t=HP)
        bmask = nsb("bmask", [P, P])
        lmax = nsb("lmax", [P, 2, MT, 8])
        lsum = nsb("lsum", [P, 2, MT, 8])
        lrec = nsb("lrec", [P, 2, MT, 8])
        lin.close()
        w1_raw = tsb("w1_raw", [P, 2, DT, FF])
        w2_raw = tsb("w2_raw", [P, 2, FT, D])
        b1_sb = tsb("b1_sb", [P, NE, FT])
        b2_sb = tsb("b2_sb", [NE, D])
        h_f = stage[:, 1, 0:B // 2, :].rearrange("p (t b) f -> p t (b f)", t=2)
        h_hi = tsb("h_hi", [P, FT, TOK], F32R)
        h_lo = tsb("h_lo", [P, FT, TOK], F32R)
        logit = tsb("logit", [P, MT, NE])
        top = tsb("top", [P, MT, 8])
        topi = tsb("topi", [P, MT, 8], U32)
        topf = tsb("topf", [P, MT, 2])
        tdiff = tsb("tdiff", [P, MT])
        texp = tsb("texp", [P, MT])
        tw = tsb("tw", [P, MT, 2])
        sel = tsb("sel", [P, MT, NE])
        gw = tsb("gw", [P, MT, NE])
        gwT = lnT[0:NE, 0, :]
        eidx = tsb("eidx", [P, NE])
        tail.close()

        sps = es.enter_context(nc.psum_tensor("sps", [P, 2, 512], F32))
        scp = es.enter_context(nc.psum_tensor("scp", [P, GT, 512], F32))
        wps = es.enter_context(nc.psum_tensor("wps", [P, 2, 512], F32))
        trp = [sps[:, 0, :], sps[:, 1, :]]
        up, wp = wps[:, 0, :], wps[:, 1, :]

        x_in = sem("x_in")
        small_in = sem("small_in")
        pw_in = sem("pw_in")
        tw_in = sem("tw_in")
        lw_in = sem("lw_in")
        raw_in = [sem(f"raw_in{i}") for i in range(RR)]
        qk_out = [sem(f"qk_out{i}") for i in range(2)]
        ident_ok = sem("ident_ok")
        pool_step = sem("pool_step")
        split_hi = sem("split_hi")
        ones_ok = sem("ones_ok")
        split_ok = sem("split_ok")
        dve_step = sem("dve_step")
        var_ok = sem("var_ok")
        sd_ok = sem("sd_ok")
        xn_ok = sem("xn_ok")
        pro_tr = sem("pro_tr")
        pro_trc = sem("pro_trc")
        pro_q = sem("pro_q")
        pro_qc = sem("pro_qc")
        pro_k = sem("pro_k")
        pro_kc_act = sem("pro_kc_act")
        pro_kc_dve = sem("pro_kc_dve")
        scores_ok = sem("scores_ok")
        out_ok = sem("out_ok")
        max_ok = sem("max_ok")
        mbc_ok = sem("mbc_ok")
        sub_ok = sem("sub_ok")
        exp_ok = sem("exp_ok")
        hi_ok = sem("hi_ok")
        lo_ok = sem("lo_ok")
        pv_ok = sem("pv_ok")
        rsum_ok = sem("rsum_ok")
        u_ok = sem("u_ok")
        ut_ok = sem("ut_ok")
        utc_ok = sem("utc_ok")
        wv_ok = sem("wv_ok")
        o_ok = sem("o_ok")
        tanh_ok = sem("tanh_ok")
        tp = sem("tp")
        ta = sem("ta")
        tv = sem("tv")
        tq = sem("tq")
        wraw_in = [sem(f"wraw_in{i}") for i in range(2)]
        w_ready = sem("w_ready")
        h_ok = sem("h_ok")
        hf_ok = sem("hf_ok")
        hh_ok = sem("hh_ok")
        hl_ok = sem("hl_ok")
        y_ok = sem("y_ok")
        yc_ok = sem("yc_ok")
        y_stage = sem("y_stage")
        stored = sem("stored")

        def fixed(v):
            return isinstance(v, int) and v <= 0

        def wait(eng, s, v):
            if not fixed(v):
                eng.wait_ge(s, v)

        def hbank(f):
            return [trp[0], trp[1], up, wp][f % 4]

        def b1_ap(i, s, f):
            if isinstance(i, int):
                e = i * 2 + s
                return b1_sb[:, e, f:f + 1]
            return b1_sb[:].rearrange("p e f -> p (e f)")[:, bass.ds(i * (2 * FT) + (s * FT + f), 1)]

        block = es.enter_context(nc.Block())

        @block.sync
        def _(sp):
            for m in range(MT):
                sp.dma_start(x_sb[:, m, :], x[P * m:P * (m + 1), :]).then_inc(x_in, 16)
            sp.dma_start(gamma_b[:], gamma.partition_broadcast(P)).then_inc(small_in, 16)
            sp.dma_start(beta_b[:], beta.partition_broadcast(P)).then_inc(small_in, 16)
            sp.dma_start(wq_sb[:], w_q.rearrange("(t p) n -> p t n", p=P)).then_inc(pw_in, 16)
            sp.dma_start(wkt_sb[:], w_kt.rearrange("(t p) n -> p t n", p=P)).then_inc(pw_in, 16)

            def load_ctx_t(count, r, b, j):
                wait(sp, split_ok, count)
                w = P if j < SJ - 1 else SL
                src = ctx_t[b, :, P * j:P * j + w].rearrange("(t p) s -> p t s", p=P)
                sp.dma_start(raw[:, r, :, 0:w], src).then_inc(raw_in[r], 16)

            ctx_rows = ctx_n.rearrange("b s d -> (b s) d")

            def load_ctx(count, r, b, j):
                wait(sp, split_ok, count)
                w = P if j < SJ - 1 else SL
                sp.dma_start(raw[0:w, r, :, :].rearrange("p t f -> p (t f)"),
                             ctx_rows[bass.ds(b * S + P * j, w), :]).then_inc(raw_in[r], 16)

            def load_qk(count, r, n):
                wait(sp, split_ok, count)
                sp.dma_start(raw[:, r, :, :].rearrange("p t f -> p (t f)"), qk_dram[n, :, :]).then_inc(raw_in[r], 16)

            def load_job(job, i):
                no = lambda q: JOB_NO[shift(job, q)]
                count = linear(i, lambda q: no(q) - RR + 1)
                r = no(1 if not isinstance(i, int) else i) % RR
                if job[0] == "ctx":
                    b = linear(i, lambda q: shift(job, q)[1] // (2 * SJ))
                    c, j = job[1] // SJ, job[1] % SJ
                    (load_ctx if c % 2 else load_ctx_t)(count, r, b, j)
                else:
                    load_qk(count, r, linear(i, lambda q: shift(job, q)[1] * GT + job[2]))

            for job in FIRST_JOBS[0:SJ]:
                load_job(job, 0)
            sp.dma_start(wv_sb[:], w_v.rearrange("(t p) n -> p t n", p=P)).then_inc(tw_in, 16)
            sp.dma_start(wout_sb[:], w_out.rearrange("(t p) n -> p t n", p=P)).then_inc(tw_in, 16)
            sp.dma_start(wo_sb[:], Wo.rearrange("(t p) n -> p t n", p=P)).then_inc(tw_in, 16)
            sp.dma_start(wr_sb[:], W_router.rearrange("(t p) n -> p t n", p=P)).then_inc(tw_in, 16)
            sp.dma_start(br_b[:], b_router.partition_broadcast(P)).then_inc(tw_in, 16)
            sp.dma_start(bout_b[:], b_out.partition_broadcast(P)).then_inc(tw_in, 16)
            sp.dma_start(bo_b[:], bo.partition_broadcast(P)).then_inc(tw_in, 16)
            sp.dma_start(tg[:, 0:1], gate.partition_broadcast(P)).then_inc(tw_in, 16)
            qk_v = qk_dram.rearrange("(b t) p f -> t p b f", t=TPB)
            for t in range(TPB):
                sp.wait_ge(pro_kc_act, 2 * (t + 1))
                sp.wait_ge(pro_kc_dve, 2 * (t + 1))
                sp.dma_start(qk_v[t], stage[:, t % 2, :, :]).then_inc(qk_out[t % 2], 16)
                if t == GT - 1:
                    for i in range(2):
                        sp.wait_ge(qk_out[i], 16 * GT // 2)
                    for job in FIRST_JOBS[SJ:]:
                        load_job(job, 0)
            for i in range(2):
                sp.wait_ge(qk_out[i], 16 * TPB // 2)

            def load_pass(i, of):
                for u in range(PASS):
                    for job in slot_jobs(of * PASS + u):
                        load_job(shift(job, -of), i)

            load_pass(0, 0)
            with sp.Fori(0, NPASS - 2) as i:
                load_pass(i, 1)
            load_pass(NPASS - 1, NPASS - 1)

            sp.wait_ge(o_ok, NG)
            for i, w in enumerate((Wq, Wk, Wv)):
                sp.dma_start(lw_sb[:, i, :, :], w.rearrange("(t p) n -> p t n", p=P)).then_inc(lw_in, 16)
            sp.wait_ge(tp, LIN_PE)
            sp.wait_ge(tv, LIN_DVE)
            sp.dma_start(b1_sb[:], b1).then_inc(small_in, 16)
            sp.dma_start(b2_sb[:], b2).then_inc(small_in, 16)

            def load_expert(e, i, s):
                wait(sp, w_ready, (i * 2 + s - 1) * 3)
                sp.dma_start(w1_raw[:, s, :, :], W1[e].rearrange("(t p) n -> p t n", p=P)).then_inc(wraw_in[s], 16)
                sp.dma_start(w2_raw[:, s, :, :], W2[e].rearrange("(t p) n -> p t n", p=P)).then_inc(wraw_in[s], 16)

            load_expert(0, 0, 0)
            load_expert(1, 0, 1)
            with sp.Fori(1, NE // 2) as i:
                load_expert(i * 2, i, 0)
                load_expert(i * 2 + 1, i, 1)
            for m in range(MT):
                sp.wait_ge(yc_ok, (NE - 1) * MT + m + 1)
                sp.dma_start(out[P * m:P * (m + 1), :], xa[:, m, :]).then_inc(stored, 16)
            sp.wait_ge(stored, 16 * MT)

        @block.gpsimd
        def _(pool):
            steps = [0]

            def link(ins):
                steps[0] += 1
                ins.then_inc(pool_step, 1)
                pool.wait_ge(pool_step, steps[0])

            link(pool.memset(ident[:], 0.0))
            link(pool.memset(zero[:], 0.0))
            pool.affine_select(out=ident[:], in_=ident[:], compare_op=ALU.not_equal, fill=1.0, base=0,
                               pattern=[[-1, P]], channel_multiplier=1).then_inc(ident_ok, 1)
            for j in range(SJ):
                last = pool.memset(cn[:, j, D:D + 2].bitcast(F32), 1.0)
            last.then_inc(ones_ok, 1)

            def split(src, hi, lo, hi_count, done):
                z = zero[0:src.shape[0], :]
                for _ in range(len(src.shape) - 2):
                    z = z.unsqueeze(1)
                pool.tensor_tensor(hi, src, z.broadcast_to(tuple(src.shape)), ALU.add).then_inc(split_hi, 1)
                pool.wait_ge(split_hi, hi_count + 1)
                pool.tensor_tensor(lo, src, hi.bitcast(F32), ALU.subtract).then_inc(done, 1)

            def split_job(job, i):
                no = linear(i, lambda q: JOB_NO[shift(job, q)])
                n1 = JOB_NO[shift(job, 1 if not isinstance(i, int) else i)]
                r = n1 % RR
                pool.wait_ge(raw_in[r], linear(i, lambda q: (JOB_NO[shift(job, q)] // RR + 1) * 16))
                if job[0] == "qk":
                    wait(pool, scores_ok, linear(i, lambda q: (shift(job, q)[1] - 1) * SJ))
                    slot = job[1] % 2
                    cols = slice(job[2] * P, (job[2] + 1) * P)
                    split(raw[:, r, :, :], qk_hi[:, slot, :, cols], qk_lo[:, slot, :, cols], no, split_ok)
                    return
                j = job[1] % SJ
                w = P if j < SJ - 1 else SL
                if job[1] // SJ % 2 == 0:
                    wait(pool, scores_ok, linear(i, lambda q: shift(job, q)[1] - SJ + 1))
                    cols = slice(P * j, P * j + w)
                    split(raw[:, r, :, 0:w], ct_hi[:, :, cols], ct_lo[:, :, cols], no, split_ok)
                else:
                    wait(pool, pv_ok, linear(i, lambda q: shift(job, q)[1] - 2 * SJ + 1))
                    src = raw[0:w, r, :, :].rearrange("p t f -> p (t f)")
                    split(src, cn[0:w, j, 0:D], cn[0:w, j, D + 2:CNW], no, split_ok)

            def all_max(g, par):
                pool.wait_ge(max_ok, (g + 1) * SJ)
                pool.tensor_tensor(mtouch[:], cmax[:, par, 0:1], zero[:], ALU.add)
                pool.partition_all_reduce(mbc[:, par, :], cmax[:, par, :], P, bass.bass_isa.ReduceOp.max)\
                    .then_inc(mbc_ok, 1)

            def split_pass(i, of):
                for u in range(PASS):
                    if u % SJ == 0 and not (of == 0 and u == 0):
                        all_max(linear(i, lambda q: q * (PASS // SJ) + u // SJ - 1), (u // SJ - 1) % 2)
                    for job in slot_jobs(of * PASS + u):
                        split_job(shift(job, -of), i)

            for job in FIRST_JOBS:
                split_job(job, 0)
            split_pass(0, 0)
            with pool.Fori(0, NPASS - 2) as i:
                split_pass(i, 1)
            split_pass(NPASS - 1, NPASS - 1)
            all_max(NG - 1, (NG - 1) % 2)
            hc = len(JOBS)

            pool.wait_ge(tp, OUT_PE)
            pool.iota(eidx[:], pattern=[[1, NE]], base=0, channel_multiplier=0,
                      allow_small_or_imprecise_dtypes=True).then_inc(tq, 1)
            hc_e = hc

            def split_expert(i, s, hc):
                pool.wait_ge(wraw_in[s], 32 * (i + 1))
                wait(pool, y_ok, (i * 2 + s - 1) * FT)
                for dt in range(DT):
                    split(w1_raw[:, s, dt, :], w1_hi[:, s, dt, :], w1_lo[:, s, dt, :], hc + dt, w_ready)
                split(w2_raw[:, s, :, :], w2_sp[:, s, :, 0:D], w2_sp[:, s, :, D:2 * D], hc + DT, w_ready)

            split_expert(0, 0, hc_e)
            split_expert(0, 1, hc_e + 3)
            with pool.Fori(1, NE // 2) as i:
                split_expert(i, 0, i * 6 + hc_e)
                split_expert(i, 1, i * 6 + (hc_e + 3))

        @block.scalar
        def _(act):
            for r in range(2):
                act.wait_ge(var_ok, r + 1)
                act.activation(sd[:], mv[:, :, 1], ACT.Sqrt).then_inc(sd_ok, 1)
            for dt in range(DT):
                act.wait_ge(pro_tr, dt + 1)
                act.activation(xnT[:, dt, :], trp[dt], ACT.Copy).then_inc(pro_trc, 1)
            for t in range(TPB):
                act.wait_ge(pro_q, t + 1)
                act.activation(qT[:, t, :], scp[:, t % GT, :], ACT.Copy, scale=float(DH) ** -0.5).then_inc(pro_qc, 1)
            for t in range(TPB):
                if t >= 2:
                    act.wait_ge(qk_out[t % 2], 16 * (t // 2))
                for dt in range(DT):
                    act.wait_ge(pro_k, DT * t + dt + 1)
                    act.activation(stage[:, t % 2, :, dt * P:dt * P + Q],
                                   scp[:, 2 * dt, :].rearrange("p (b q) -> p b q", q=Q),
                                   ACT.Copy).then_inc(pro_kc_act, 1)

            def rows(j):
                return P if j < SJ - 1 else SL

            def take_scores(i, u):
                j, par = u % SJ, u // SJ % 2
                act.wait_ge(scores_ok, linear(i, lambda q: q * PASS + u + 1))
                act.activation(st[0:rows(j), par, j, :], sps[0:rows(j), u % 2, :], ACT.Copy).then_inc(out_ok, 1)

            def exps(i, u):
                j, par, r = u % SJ, u // SJ % 2, u % PR
                p = st[0:rows(j), par, j, :]
                act.wait_ge(sub_ok, linear(i, lambda q: q * PASS + u + 1))
                act.activation(p, p, ACT.Exp).then_inc(exp_ok, 1)
                act.wait_ge(exp_ok, linear(i, lambda q: q * PASS + u + 1))
                wait(act, pv_ok, linear(i, lambda q: q * PASS + u - PR + 1))
                act.activation(pt_hi[0:rows(j), r, :], p, ACT.Copy).then_inc(hi_ok, 1)

            def take_ut(i, u):
                for x in range(2):
                    act.wait_ge(ut_ok, linear(i, lambda q: (q * (PASS // SJ) + u // SJ - 2) * 2 + x + 1))
                    if x == 0:
                        wait(act, wv_ok, linear(i, lambda q: q * (PASS // SJ) + u // SJ - 2))
                    act.activation(ut_sb[:, 2 * x:2 * x + 2, :, :],
                                   wps[:, x, :].rearrange("p (a t q) -> p a t q", a=2, t=DT), ACT.Copy).then_inc(utc_ok, 1)

            def slot(i, u, k):
                if 1 <= k <= NSLOT:
                    take_scores(i, u - 1)
                if L_SUB <= k < NSLOT + L_SUB:
                    exps(i, u - L_SUB)
                if u % SJ == V_UTC and k >= 2 * SJ:
                    take_ut(i, u)

            for u in range(PASS):
                slot(0, u, u)
            with act.Fori(0, NPASS - 1) as i:
                for u in range(PASS):
                    slot(i, u, PASS + u)
            for k in range(NSLOT, (NG + 1) * SJ + V_O + 1):
                slot(0, k, k)

            act.wait_ge(tw_in, 16 * 8)
            act.activation(tg[:, 1:2], tg[:, 0:1], ACT.Tanh).then_inc(tanh_ok, 1)
            n = [0]

            def done(ins):
                n[0] += 1
                ins.then_inc(ta, 1)

            act.wait_ge(tv, V_VAR1)
            done(act.activation(sd[:], mv[:, :, 1], ACT.Sqrt))
            act.wait_ge(tp, PT_LN1)
            done(act.activation(lnT[:, 0, :], trp[0], ACT.Copy))
            for m in range(MT):
                act.wait_ge(tp, PT_V + m + 1)
                done(act.activation(v_sb[:, m, :], scp[:, m, :], ACT.Copy))
            act.wait_ge(tv, V_KSUB)
            done(act.activation(ke[:], ke[:], ACT.Exp))
            act.wait_ge(tv, V_QSUB)
            done(act.activation(qe[:], qe[:], ACT.Exp))
            for m in range(0, MT, 2):
                act.wait_ge(tp, PT_KT + m + 1)
                done(act.activation(kn[:, m, :], scp[:, m, :], ACT.Copy))
            for m in range(0, HP, 2):
                act.wait_ge(tp, PT_QT + m + 1)
                done(act.activation(lqT[:, m, :], [trp[0], trp[1], up, wp][m], ACT.Copy))
            for t in range(HP):
                act.wait_ge(tp, PT_OT)
                done(act.activation(lo_T[:, t, :], scp[:, t, :], ACT.Copy))
            act.wait_ge(tv, V_VAR2)
            done(act.activation(sd[:], mv[:, :, 1], ACT.Sqrt))
            act.wait_ge(tp, PT_LN2)
            for dt in range(DT):
                done(act.activation(lnT_hi[:, dt, :], trp[dt], ACT.Copy))
            act.wait_ge(tv, V_TDIFF)
            done(act.activation(texp[:], tdiff[:], ACT.Exp))

            def expert(i, s):
                for f in range(FT):
                    k = (i * 2 + s) * FT + f
                    act.wait_ge(h_ok, k + 1)
                    wait(act, hl_ok, k - 1)
                    act.activation(h_f[:, f % 2, :], hbank(f), ACT.Relu,
                                   bias=b1_ap(i, s, f)).then_inc(hf_ok, 1)
            act.wait_ge(small_in, 64)
            expert(0, 0)
            expert(0, 1)
            with act.Fori(1, NE // 2) as i:
                expert(i, 0)
                expert(i, 1)

        @block.vector
        def _(dve):
            steps = [0]

            def link(ins):
                steps[0] += 1
                ins.then_inc(dve_step, 1)
                dve.wait_ge(dve_step, steps[0])

            def norm_stats(src, m):
                link(dve.bn_stats(stats[:, m, :], src))
                link(dve.bn_aggr(mv[:, m, :], stats[:, m, :]))

            for r in range(2):
                for m in range(MT):
                    if r == 0:
                        dve.wait_ge(x_in, 16 * MT)
                    norm_stats(x_sb[:, m, :] if r == 0 else xn[:, m, :], m)
                dve.tensor_scalar(mv[:, :, 1], mv[:, :, 1], EPS, None, ALU.add).then_inc(var_ok, 1)
                dve.wait_ge(sd_ok, r + 1)
                link(dve.reciprocal(rstd[:], sd[:]))
                for m in range(MT):
                    src = x_sb[:, m, :] if r == 0 else xn[:, m, :]
                    link(dve.tensor_scalar(xn[:, m, :], src, mv[:, m, 0:1], rstd[:, m:m + 1],
                                           ALU.subtract, ALU.mult))
            dve.wait_ge(small_in, 32)
            for m in range(MT):
                link(dve.tensor_tensor(xn[:, m, :], xn[:, m, :], gamma_b[:], ALU.mult))
                dve.tensor_tensor(xn[:, m, :], xn[:, m, :], beta_b[:], ALU.add).then_inc(xn_ok, 1)
            for t in range(TPB):
                if t >= 2:
                    dve.wait_ge(qk_out[t % 2], 16 * (t // 2))
                for dt in range(DT):
                    dve.wait_ge(pro_k, DT * t + dt + 1)
                    dve.tensor_copy(stage[:, t % 2, :, dt * P + Q:(dt + 1) * P],
                                    scp[:, 2 * dt + 1, :].rearrange("p (b q) -> p b q", q=Q)).then_inc(pro_kc_dve, 1)

            def rows(j):
                return P if j < SJ - 1 else SL

            def minus_max(i, u):
                j, par = u % SJ, u // SJ % 2
                p = st[0:rows(j), par, j, :]
                dve.wait_ge(out_ok, linear(i, lambda q: q * PASS + u + 1))
                if j == 0:
                    dve.wait_ge(mbc_ok, linear(i, lambda q: q * (PASS // SJ) + u // SJ + 1))
                dve.tensor_tensor(p, p, mbc[0:rows(j), par, :], ALU.subtract).then_inc(sub_ok, 1)

            def running_max(i, u):
                j, par = u % SJ, u // SJ % 2
                dve.wait_ge(out_ok, linear(i, lambda q: q * PASS + u + 1))
                src = st[0:rows(j), par, j, :]
                m = cmax[0:rows(j), par, :]
                if j == 0:
                    dve.tensor_copy(m, src).then_inc(max_ok, 1)
                else:
                    dve.wait_ge(max_ok, linear(i, lambda q: q * PASS + u))
                    dve.tensor_tensor(m, m, src, ALU.max).then_inc(max_ok, 1)

            def low_part(i, u):
                j, par, r = u % SJ, u // SJ % 2, u % PR
                dve.wait_ge(hi_ok, linear(i, lambda q: q * PASS + u + 1))
                dve.tensor_tensor(pt_lo[0:rows(j), r, :], st[0:rows(j), par, j, :],
                                  pt_hi[0:rows(j), r, :].bitcast(F32), ALU.subtract).then_inc(lo_ok, 1)

            def take_u(i, u):
                for t in range(GT):
                    g = linear(i, lambda q: (q * (PASS // SJ) + u // SJ - 2) * GT + t)
                    if t == 0:
                        dve.wait_ge(pv_ok, linear(i, lambda q: (q * (PASS // SJ) + u // SJ - 1) * SJ))
                        wait(dve, ut_ok, linear(i, lambda q: (q * (PASS // SJ) + u // SJ - 2) * 2))
                    dve.reciprocal(rsum[:, t:t + 1], scp[:, t, D:D + 1]).then_inc(rsum_ok, 1)
                    dve.wait_ge(rsum_ok, g + 1)
                    dve.tensor_scalar(u_sb[:, t, :], scp[:, t, 0:D], rsum[:, t:t + 1], None, ALU.mult).then_inc(u_ok, 1)

            def take_o(i, u, tok):
                half = u // SJ % GPB
                ts_ = slice(half * GT, (half + 1) * GT)
                v = wps[:, 0, :].rearrange("p (t q) -> p t q", t=GT)
                dve.wait_ge(wv_ok, linear(i, lambda q: q * (PASS // SJ) + u // SJ - 1))
                dve.tensor_copy(oT[0:Q, ts_, tok], v[0:Q, :, 0:Q])
                dve.tensor_copy(oT[Q:P, ts_, tok], v[Q:P, :, Q:P]).then_inc(o_ok, 1)

            def slot(i, u, k):
                if u % SJ == V_U and k >= 2 * SJ:
                    take_u(i, u)
                if L_SUB <= k < NSLOT + L_SUB:
                    minus_max(i, u - L_SUB)
                if L_LO <= k < NSLOT + L_LO:
                    low_part(i, u - L_LO)
                if 1 <= k <= NSLOT:
                    running_max(i, u - 1)
                if u % SJ == V_O and k >= 2 * SJ:
                    b = u // (2 * SJ) - 1
                    if isinstance(i, int):
                        take_o(i, u, slice((i * 2 + b) * Q, (i * 2 + b + 1) * Q))
                    else:
                        take_o(i, u, bass.ds(i * (2 * Q) + (b + 2) * Q, Q))

            for u in range(PASS):
                slot(0, u, u)
            with dve.Fori(0, NPASS - 1) as i:
                for u in range(PASS):
                    slot(i, u, PASS + u)
            for k in range(NSLOT, (NG + 1) * SJ + V_O + 1):
                slot(0, k, k)

            n = [0]

            def done(ins):
                n[0] += 1
                ins.then_inc(tv, 1)

            def then(ins):
                done(ins)
                dve.wait_ge(tv, n[0])

            def at(want, name):
                assert n[0] == want, (name, n[0], want)

            def layer_norm(src, act_count):
                for m in range(MT):
                    then(dve.bn_stats(stats[:, m, :], src[:, m, :]))
                    then(dve.bn_aggr(mv[:, m, :], stats[:, m, :]))
                then(dve.tensor_scalar(mv[:, :, 1], mv[:, :, 1], EPS, None, ALU.add))
                dve.wait_ge(ta, act_count)
                then(dve.reciprocal(rstd[:], sd[:]))
                for m in range(MT):
                    done(dve.tensor_scalar(ln_out[:, m, :], src[:, m, :], mv[:, m, 0:1], rstd[:, m:m + 1],
                                           ALU.subtract, ALU.mult))

            dve.wait_ge(tw_in, 16 * 8)
            dve.wait_ge(tanh_ok, 1)
            for m in range(MT):
                dve.wait_ge(tp, m + 1)
                then(dve.tensor_tensor(xa[:, m, :], scp[:, m, 0:D], bout_b[:], ALU.add))
                then(dve.scalar_tensor_tensor(out=x1[:, m, :], in0=xa[:, m, :], scalar=tg[:, 1:2], in1=x_sb[:, m, :],
                                              op0=ALU.mult, op1=ALU.add))
            layer_norm(x1, 1)
            at(V_LN1, "V_LN1")
            dve.wait_ge(tp, PT_LN1)
            done(dve.tensor_copy(lnT[:, 1, :], trp[1]))
            at(V_LNT1, "V_LNT1")
            done(dve.memset(cbd[:].rearrange("p b t e -> p (b t e)"), 0.0))
            then(dve.memset(bmask[:], 0.0))
            done(dve.memset(bmask[0:Q, 0:Q], 1.0))
            done(dve.memset(bmask[Q:P, Q:P], 1.0))
            for t in range(HP):
                dve.wait_ge(tp, PT_K + t + 1)
                ps = scp[:, t, :].rearrange("p (b n) -> p b n", n=Q)
                then(dve.tensor_reduce(lmax[:, 0, t, :], ps, AX.X, ALU.max))
                done(dve.tensor_tensor(ke[:, t, :].rearrange("p (b n) -> p b n", n=Q), ps,
                                       lmax[:, 0, t, :].unsqueeze(2).broadcast_to((P, 8, Q)), ALU.subtract))
            at(V_KSUB, "V_KSUB")
            for m in range(MT):
                dve.wait_ge(tp, PT_Q + m + 1)
                ps = [trp[0], trp[1], up, wp][m].rearrange("p (b n) -> p b n", n=LD)
                then(dve.tensor_reduce(lmax[:, 1, m, :], ps, AX.X, ALU.max))
                done(dve.tensor_tensor(qe[:, m, :].rearrange("p (b n) -> p b n", n=LD), ps,
                                       lmax[:, 1, m, :].unsqueeze(2).broadcast_to((P, 8, LD)), ALU.subtract))
            at(V_QSUB, "V_QSUB")
            for w, (buf, cnt) in enumerate(((ke, 7), (qe, 8))):
                dve.wait_ge(ta, cnt)
                v3 = buf[:].rearrange("p t (b n) -> p (t b) n", n=Q)
                r2 = lrec[:, w, :, :].rearrange("p t b -> p (t b)")
                then(dve.tensor_reduce(lsum[:, w, :, :].rearrange("p t b -> p (t b)"), v3, AX.X, ALU.add))
                then(dve.reciprocal(r2, lsum[:, w, :, :].rearrange("p t b -> p (t b)")))
                if w == 1:
                    then(dve.tensor_scalar(r2, r2, float(LD) ** -0.5, None, ALU.mult))
                done(dve.tensor_tensor(v3, v3, r2.unsqueeze(2).broadcast_to((P, 32, Q)), ALU.mult))
                at((V_KN, V_QN)[w], "V_KN/V_QN")
            for m in range(1, MT, 2):
                dve.wait_ge(tp, PT_KT + m + 1)
                done(dve.tensor_copy(kn[:, m, :], scp[:, m, :]))
            for m in range(1, HP, 2):
                dve.wait_ge(tp, PT_QT + m + 1)
                done(dve.tensor_copy(lqT[:, m, :], [trp[0], trp[1], up, wp][m]))
            at(V_QTC, "V_QTC")
            for b in range(B):
                dve.wait_ge(tp, PT_CTX + b + 1)
                done(dve.tensor_tensor(cbd[:, b, :, :], [trp[0], trp[1], up, wp][b % 4].rearrange("p (t e) -> p t e", e=P),
                                       bmask[:].unsqueeze(1).broadcast_to((P, HP, P)), ALU.mult))
            at(V_CBD, "V_CBD")
            for m in range(MT):
                dve.wait_ge(tp, PT_Y + m + 1)
                then(dve.tensor_tensor(xa[:, m, :], scp[:, m, 0:D], bo_b[:], ALU.add))
                then(dve.tensor_tensor(xa[:, m, :], xa[:, m, :], x1[:, m, :], ALU.add))
            layer_norm(xa, 17)
            at(V_LN2, "V_LN2")
            dve.wait_ge(tp, PT_LN2)
            dve.wait_ge(ta, 19)
            for dt in range(DT):
                done(dve.tensor_tensor(lnT_lo[:, dt, :], trp[dt], lnT_hi[:, dt, :].bitcast(F32), ALU.subtract))
            for dt in range(DT):
                done(dve.tensor_copy(lnT[:, dt, :], trp[dt]))
            at(V_LNT2, "V_LNT2")
            dve.wait_ge(tp, PT_R)
            for m in range(MT):
                then(dve.tensor_tensor(logit[:, m, :], up[:, m * NE:(m + 1) * NE], br_b[:], ALU.add))
                then(dve.max(top[:, m, :], logit[:, m, :]))
                then(dve.max_index(topi[:, m, :], top[:, m, :], logit[:, m, :]))
            done(dve.tensor_copy(topf[:], topi[:, :, 0:2]))
            done(dve.tensor_tensor(tdiff[:], top[:, :, 1], top[:, :, 0], ALU.subtract))
            at(V_TDIFF, "V_TDIFF")
            dve.wait_ge(tv, n[0])
            dve.wait_ge(ta, 20)
            then(dve.tensor_scalar(sd[:], texp[:], 1.0, None, ALU.add))
            then(dve.reciprocal(tw[:, :, 0], sd[:]))
            then(dve.tensor_tensor(tw[:, :, 1], tw[:, :, 0], texp[:], ALU.mult))
            dve.wait_ge(tq, 1)
            for m in range(MT):
                then(dve.tensor_scalar(gw[:, m, :], eidx[:], topf[:, m, 0:1], tw[:, m, 0:1], ALU.is_equal, ALU.mult))
                then(dve.tensor_scalar(sel[:, m, :], eidx[:], topf[:, m, 1:2], tw[:, m, 1:2], ALU.is_equal, ALU.mult))
                then(dve.tensor_tensor(gw[:, m, :], gw[:, m, :], sel[:, m, :], ALU.add))
            at(V_GW, "V_GW")
            dve.wait_ge(tp, PT_GT)
            done(dve.tensor_copy(gwT[:], up[0:NE, :]))
            at(V_GWT, "V_GWT")
            for m in range(MT):
                dve.wait_ge(tp, PT_B2)
                then(dve.tensor_tensor(xa[:, m, :], xa[:, m, :], scp[:, m, 0:D], ALU.add))
            at(V_B2, "V_B2")

            def gate_ap(i, s, m):
                if isinstance(i, int):
                    return gw[:, m, i * 2 + s:i * 2 + s + 1]
                return gw[:].rearrange("p m e -> p (m e)")[:, bass.ds(i * 2 + (m * NE + s), 1)]

            def expert(i, s):
                for f in range(FT):
                    k = (i * 2 + s) * FT + f
                    dve.wait_ge(hf_ok, k + 1)
                    wait(dve, y_ok, k - (FT - 1))
                    dve.tensor_copy(h_hi[:, f, :], h_f[:, f % 2, :]).then_inc(hh_ok, 1)
                    dve.wait_ge(hh_ok, k + 1)
                    dve.tensor_tensor(h_lo[:, f, :], h_f[:, f % 2, :], h_hi[:, f, :].bitcast(F32),
                                      ALU.subtract).then_inc(hl_ok, 1)
                for m in range(MT):
                    k = (i * 2 + s) * MT + m
                    dve.wait_ge(y_ok, (i * 2 + s + 1) * FT)
                    dve.scalar_tensor_tensor(out=xa[:, m, :], in0=scp[:, m, 0:D], scalar=gate_ap(i, s, m),
                                             in1=xa[:, m, :], op0=ALU.mult, op1=ALU.add).then_inc(y_stage, 1)
                    dve.wait_ge(y_stage, k + 1)
                    dve.scalar_tensor_tensor(out=xa[:, m, :], in0=scp[:, m, D:2 * D], scalar=gate_ap(i, s, m),
                                             in1=xa[:, m, :], op0=ALU.mult, op1=ALU.add).then_inc(yc_ok, 1)

            expert(0, 0)
            expert(0, 1)
            with dve.Fori(1, NE // 2) as i:
                expert(i, 0)
                expert(i, 1)

        @block.tensor
        def _(pe):
            pe.wait_ge(ident_ok, 1)
            pe.wait_ge(xn_ok, MT)
            for dt in range(DT):
                for m in range(MT):
                    ins = pe.transpose(trp[dt][:, m * P:(m + 1) * P], xn[:, m, dt * P:(dt + 1) * P], ident[:])
                ins.then_inc(pro_tr, 1)
            pe.wait_ge(pw_in, 32)
            pe.wait_ge(pro_trc, DT)
            for t in range(TPB):
                if t >= GT:
                    pe.wait_ge(pro_qc, t - GT + 1)
                for dt in range(DT):
                    ins = pe.matmul(scp[:, t % GT, :], wq_sb[:, dt, t * P:(t + 1) * P], xnT[:, dt, :],
                                    start=dt == 0, stop=dt == DT - 1)
                ins.then_inc(pro_q, 1)
            pe.wait_ge(pro_qc, TPB)
            for t in range(TPB):
                for dt in range(DT):
                    if t >= 1:
                        pe.wait_ge(pro_kc_act, DT * (t - 1) + dt + 1)
                        pe.wait_ge(pro_kc_dve, DT * (t - 1) + dt + 1)
                    for par in range(2):
                        rows = slice(par * Q, (par + 1) * Q)
                        ins = pe.matmul(scp[:, 2 * dt + par, :], wkt_sb[rows, t, dt * P:(dt + 1) * P], qT[rows, t, :],
                                        start=True, stop=True)
                    ins.then_inc(pro_k, 1)

            def rows(j):
                return P if j < SJ - 1 else SL

            def scores(i, u):
                j, par = u % SJ, u // SJ % 2
                w = 2 * SJ * (u // (2 * SJ)) + j
                need = [("ctx", w)]
                if j == 0:
                    need.append(("qk", u // SJ, GT - 1))
                pe.wait_ge(split_ok, linear(i, lambda q: max(JOB_NO[shift(n, q)] for n in need) + 1))
                wait(pe, out_ok, linear(i, lambda q: q * PASS + u - 1))
                cols = slice(P * j, P * j + rows(j))
                c = 0
                for dt in range(DT):
                    for a, v in ((ct_hi, qk_hi), (ct_hi, qk_lo), (ct_lo, qk_hi)):
                        ins = pe.matmul(sps[0:rows(j), u % 2, :], a[:, dt, cols], v[:, par, dt, :],
                                        start=c == 0, stop=c == 5)
                        c += 1
                ins.then_inc(scores_ok, 1)

            def times_context(i, u):
                j, r = u % SJ, u % PR
                pe.wait_ge(lo_ok, linear(i, lambda q: q * PASS + u + 1))
                w = 2 * SJ * (u // (2 * SJ)) + SJ + j
                pe.wait_ge(split_ok, linear(i, lambda q: JOB_NO[shift(("ctx", w), q)] + 1))
                for t in range(GT):
                    if j == 0:
                        wait(pe, u_ok, linear(i, lambda q: (q * (PASS // SJ) + u // SJ - 1) * GT + t + 1))
                    cols = slice(t * P, (t + 1) * P)
                    hi, lo = pt_hi[0:rows(j), r, cols], pt_lo[0:rows(j), r, cols]
                    pe.matmul(scp[:, t, 0:D + 2], hi, cn[0:rows(j), j, 0:D + 2], start=j == 0, stop=False)
                    pe.matmul(scp[:, t, 0:D], hi, cn[0:rows(j), j, D + 2:CNW], start=False, stop=False)
                    ins = pe.matmul(scp[:, t, 0:D + 2], lo, cn[0:rows(j), j, 0:D + 2], start=False, stop=j == SJ - 1)
                ins.then_inc(pv_ok, 1)

            def transpose_u(i, u):
                for x in range(2):
                    pe.wait_ge(u_ok, linear(i, lambda q: (q * (PASS // SJ) + u // SJ - 2) * GT + 2 * x + 2))
                    if x == 0:
                        wait(pe, o_ok, linear(i, lambda q: q * (PASS // SJ) + u // SJ - 2))
                    for a in range(2):
                        for dt in range(DT):
                            ins = pe.transpose(wps[:, x, (a * DT + dt) * P:(a * DT + dt + 1) * P],
                                               u_sb[:, 2 * x + a, dt * P:(dt + 1) * P], ident[:])
                    ins.then_inc(ut_ok, 1)

            def times_wv(i, u):
                half = u // SJ % GPB
                pe.wait_ge(utc_ok, linear(i, lambda q: (q * (PASS // SJ) + u // SJ - 1) * 2))
                for t in range(GT):
                    h0 = (half * GT + t) * P
                    for dt in range(DT):
                        ins = pe.matmul(wps[:, 0, t * P:(t + 1) * P], wv_sb[:, dt, h0:h0 + P], ut_sb[:, t, dt, :],
                                        start=dt == 0, stop=dt == DT - 1)
                ins.then_inc(wv_ok, 1)

            def slot(i, u, k):
                if k < NSLOT:
                    scores(i, u)
                if L_PV <= k < NSLOT + L_PV:
                    times_context(i, u - L_PV)
                if u % SJ == V_UT and k >= 2 * SJ:
                    transpose_u(i, u)
                if u % SJ == V_WV and k >= 2 * SJ:
                    times_wv(i, u)

            pe.wait_ge(tw_in, 16 * 8)
            pe.wait_ge(ones_ok, 1)
            for u in range(PASS):
                slot(0, u, u)
            with pe.Fori(0, NPASS - 1) as i:
                for u in range(PASS):
                    slot(i, u, PASS + u)
            for k in range(NSLOT, (NG + 1) * SJ + V_O + 1):
                slot(0, k, k)

            n = [0]

            def done(ins):
                n[0] += 1
                ins.then_inc(tp, 1)

            def at(want, name):
                assert n[0] == want, (name, n[0], want)

            quad = [trp[0], trp[1], up, wp]
            pe.wait_ge(o_ok, NG)
            for m in range(MT):
                for t in range(TPB):
                    ins = pe.matmul(scp[:, m, 0:D], oT[:, t, m * P:(m + 1) * P], wout_sb[:, t, :],
                                    start=t == 0, stop=t == TPB - 1)
                done(ins)
            at(OUT_PE, "OUT_PE")
            pe.wait_ge(tv, V_LN1)
            for dt in range(DT):
                for m in range(MT):
                    ins = pe.transpose(trp[dt][:, m * P:(m + 1) * P], ln_out[:, m, dt * P:(dt + 1) * P], ident[:])
            done(ins)
            at(PT_LN1, "PT_LN1")
            pe.wait_ge(ta, 2)
            pe.wait_ge(tv, V_LNT1)
            pe.wait_ge(lw_in, 48)
            for t in range(HP):
                for dt in range(DT):
                    ins = pe.matmul(scp[:, t, :], lw_sb[:, 1, dt, t * P:(t + 1) * P], lnT[:, dt, :],
                                    start=dt == 0, stop=dt == DT - 1)
                done(ins)
            at(PT_Q, "PT_Q")
            for m in range(MT):
                for dt in range(DT):
                    ins = pe.matmul(quad[m], lnT[:, dt, m * P:(m + 1) * P], lw_sb[:, 0, dt, :],
                                    start=dt == 0, stop=dt == DT - 1)
                done(ins)
            at(PT_V, "PT_V")
            pe.wait_ge(tv, V_KSUB)
            for m in range(MT):
                for dt in range(DT):
                    ins = pe.matmul(scp[:, m, :], lnT[:, dt, m * P:(m + 1) * P], lw_sb[:, 2, dt, :],
                                    start=dt == 0, stop=dt == DT - 1)
                done(ins)
            at(PT_KT, "PT_KT")
            pe.wait_ge(ta, 6)
            pe.wait_ge(tv, V_KN)
            for m in range(MT):
                for t in range(HP):
                    ins = pe.transpose(scp[:, m, t * P:(t + 1) * P], ke[:, t, m * P:(m + 1) * P], ident[:])
                done(ins)
            at(PT_QT, "PT_QT")
            pe.wait_ge(tv, V_QN)
            for t in range(HP):
                for m in range(MT):
                    ins = pe.transpose(quad[t][:, m * P:(m + 1) * P], qe[:, m, t * P:(t + 1) * P], ident[:])
                done(ins)
            at(PT_CTX, "PT_CTX")
            pe.wait_ge(ta, 12)
            pe.wait_ge(tv, V_QTC)
            for b in range(B):
                if b >= 4:
                    pe.wait_ge(tv, V_QTC + b - 3)
                rows = slice((b % 2) * Q, (b % 2 + 1) * Q)
                for t in range(HP):
                    ins = pe.matmul(quad[b % 4][:, t * P:(t + 1) * P], kn[rows, b // 2, t * P:(t + 1) * P],
                                    v_sb[rows, b // 2, t * P:(t + 1) * P], start=True, stop=True)
                done(ins)
            at(PT_CTX + B, "ctx")
            pe.wait_ge(tv, V_CBD)
            for t in range(HP):
                for b in range(B):
                    ins = pe.matmul(scp[:, t, b * Q:(b + 1) * Q], cbd[:, b, t, :], lqT[:, t, b * Q:(b + 1) * Q],
                                    start=True, stop=True)
            done(ins)
            at(PT_OT, "PT_OT")
            pe.wait_ge(ta, 16)
            for m in range(MT):
                for t in range(HP):
                    ins = pe.matmul(scp[:, m, 0:D], lo_T[:, t, m * P:(m + 1) * P], wo_sb[:, t, :],
                                    start=t == 0, stop=t == HP - 1)
                done(ins)
            at(LIN_PE, "LIN_PE")
            pe.wait_ge(tv, V_LN2)
            for dt in range(DT):
                for m in range(MT):
                    ins = pe.transpose(trp[dt][:, m * P:(m + 1) * P], ln_out[:, m, dt * P:(dt + 1) * P], ident[:])
            done(ins)
            at(PT_LN2, "PT_LN2")
            pe.wait_ge(tv, V_LNT2)
            for m in range(MT):
                for dt in range(DT):
                    ins = pe.matmul(up[:, m * NE:(m + 1) * NE], lnT[:, dt, m * P:(m + 1) * P], wr_sb[:, dt, :],
                                    start=dt == 0, stop=dt == DT - 1)
            done(ins)
            at(PT_R, "PT_R")
            pe.wait_ge(tv, V_GW)
            for m in range(MT):
                ins = pe.transpose(up[0:NE, m * P:(m + 1) * P], gw[:, m, :], ident[:])
            done(ins)
            at(PT_GT, "PT_GT")
            pe.wait_ge(tv, V_GWT)
            pe.wait_ge(small_in, 64)
            for m in range(MT):
                ins = pe.matmul(scp[:, m, 0:D], gwT[:, m * P:(m + 1) * P], b2_sb[:], start=True, stop=True)
            done(ins)
            at(PT_B2, "PT_B2")
            pe.wait_ge(tv, V_B2)

            def expert(i, s):
                e = i * 2 + s
                for f in range(FT):
                    k = e * FT + f
                    if f == 0:
                        pe.wait_ge(w_ready, (e + 1) * 3)
                    wait(pe, hf_ok, k - 3)
                    c = 0
                    for dt in range(DT):
                        for w, v in ((w1_hi, lnT_hi), (w1_hi, lnT_lo), (w1_lo, lnT_hi)):
                            ins = pe.matmul(hbank(f), w[:, s, dt, f * P:(f + 1) * P], v[:, dt, :],
                                            start=c == 0, stop=c == 5)
                            c += 1
                    ins.then_inc(h_ok, 1)
                for f in range(FT):
                    pe.wait_ge(hl_ok, e * FT + f + 1)
                    for m in range(MT):
                        if f == 0:
                            wait(pe, yc_ok, e * MT + m - (MT - 1))
                        ms = slice(m * P, (m + 1) * P)
                        pe.matmul(scp[:, m, :], h_hi[:, f, ms], w2_sp[:, s, f, :], start=f == 0, stop=False)
                        ins = pe.matmul(scp[:, m, 0:D], h_lo[:, f, ms], w2_sp[:, s, f, 0:D],
                                        start=False, stop=f == FT - 1)
                    ins.then_inc(y_ok, 1)

            expert(0, 0)
            expert(0, 1)
            with pe.Fori(1, NE // 2) as i:
                expert(i, 0)
                expert(i, 1)


OUT_PE = MT
PT_LN1 = OUT_PE + 1
PT_K = PT_LN1
PT_Q = PT_K + HP
PT_V = PT_Q + MT
PT_KT = PT_V + MT
PT_QT = PT_KT + MT
PT_CTX = PT_QT + HP
PT_OT = PT_CTX + B + 1
PT_Y = PT_OT
LIN_PE = PT_Y + MT
PT_LN2 = LIN_PE + 1
PT_R = PT_LN2 + 1
PT_GT = PT_R + 1
PT_B2 = PT_GT + 1
V_X1 = 2 * MT
V_VAR1 = V_X1 + 2 * MT + 1
V_LN1 = V_VAR1 + 1 + MT
V_LNT1 = V_LN1 + 1
V_KSUB = V_LNT1 + 4 + 2 * HP
V_QSUB = V_KSUB + 2 * MT
V_KN = V_QSUB + 3
V_QN = V_KN + 4
V_QTC = V_QN + MT // 2 + HP // 2
V_CBD = V_QTC + B
V_X2 = V_CBD + 2 * MT
LIN_DVE = V_CBD
V_VAR2 = V_X2 + 2 * MT + 1
V_LN2 = V_VAR2 + 1 + MT
V_LNT2 = V_LN2 + 2 * DT
V_TDIFF = V_LNT2 + 3 * MT + 2
V_GW = V_TDIFF + 3 + 3 * MT
V_GWT = V_GW + 1
V_B2 = V_GWT + MT


def kernel(**inputs):
    import numpy as np
    import concourse.bacc as bacc
    from concourse.bass_utils import run_bass_kernel_spmd

    a = {k: np.asarray(v) for k, v in inputs.items()}
    inner = H * DH
    w_kv = a["L0_xattn_w_kv"]
    arrays = {
        "x": a["x"].reshape(TOK, D),
        "ctx_n": a["ctx_1024"],
        "ctx_t": a["ctx_1024"].transpose(0, 2, 1),
        "gamma": a["L0_xattn_ln_gamma"],
        "beta": a["L0_xattn_ln_beta"],
        "w_q": a["L0_xattn_w_q"],
        "w_kt": w_kv[:, :inner].T,
        "w_v": w_kv[:, inner:],
        "w_out": a["L0_xattn_w_out"],
        "b_out": a["L0_xattn_b_out"],
        "gate": a["L0_xattn_gate"],
        "Wq": a["L0_attn_Wq"], "Wk": a["L0_attn_Wk"], "Wv": a["L0_attn_Wv"], "Wo": a["L0_attn_Wo"],
        "bo": a["L0_attn_bo"],
        "W_router": a["L0_ffn_W_router"], "b_router": a["L0_ffn_b_router"],
        "W1": a["L0_ffn_W1"],
        "b1": a["L0_ffn_b1"].reshape(NE, FT, P).transpose(2, 0, 1),
        "W2": a["L0_ffn_W2"],
        "b2": a["L0_ffn_b2"],
    }
    arrays = {k: np.ascontiguousarray(v) for k, v in arrays.items()}
    nc = bacc.Bacc("TRN2", target_bir_lowering=False, num_devices=1)
    args = [nc.dram_tensor(k, v.shape, mybir.dt.from_np(v.dtype), kind="ExternalInput").ap()
            for k, v in arrays.items()]
    out = nc.dram_tensor("out", (TOK, D), F32, kind="ExternalOutput").ap()
    build(nc, *args, out)
    r = run_bass_kernel_spmd(nc, [arrays], core_ids=[0])
    return r.results[0]["out"].reshape(B, Q, D)
```

```python
from contextlib import ExitStack

import concourse.bass as bass
from concourse import mybir

F32 = mybir.dt.float32
F32R = mybir.dt.float32r
U32 = mybir.dt.uint32
ALU = mybir.AluOpType
ACT = mybir.ActivationFunctionType
AX = mybir.AxisListType

P = 128
B, Q, D = 8, 64, 256
S = 1601
H, DH = 16, 64
TOK = B * Q
MT = TOK // P
DT = D // P
TPB = H * Q // P
GT = 4
GW = GT * P
NG = B * TPB // GT
GPB = NG // B
SJ = (S + P - 1) // P
SL = S - (SJ - 1) * P
NSLOT = NG * SJ
CNW = 2 * D + 2
L_SUB, L_LO, L_PV = SJ + 4, SJ + 5, SJ + 6
PASS = 4 * SJ
NPASS = NSLOT // PASS
V_U, V_UT, V_UTC, V_WV, V_O = 5, 6, 7, 8, 9
RR = 4
PR = 4
LH, LD = 8, 64
HID = LH * LD
HP = HID // P
NE, FF = 8, 1024
FT = FF // P
EPS = 1e-5

DRAIN = (NG + 1) * SJ + V_O + 1
CHAIN_AT = [NSLOT, NSLOT + 5, NSLOT + 15, DRAIN]
CHAIN_LEN = 16
SPREAD = CHAIN_AT[2] + CHAIN_LEN
LAST = dict(zip((2, 4, 6, 7, 8, 11, 12, 14), range(SPREAD - DRAIN, CHAIN_LEN - 1)))
W_HI_AT = SPREAD - 5

UNIT_LEAD = 6


def slot_jobs(k):
    g, j = k // SJ, k % SJ
    jobs = []
    if 2 * SJ <= k + UNIT_LEAD < 2 * SJ * B:
        jobs.append(("ctx", k + UNIT_LEAD))
    if j in (1, 4, 7, 10) and g + 1 < NG:
        jobs.append(("qk", g + 1, j // 3))
    return jobs


FIRST_JOBS = [("ctx", w) for w in range(2 * SJ - 2 * GT)]
LATE_LOADS = [[("ctx", 2 * SJ - 2 * (GT - t) + x) for x in range(2)] for t in range(GT)]
FIRST_JOBS += [("qk", 0, t) for t in range(GT)] + sum(LATE_LOADS, [])
JOBS = FIRST_JOBS + [job for k in range(NSLOT) for job in slot_jobs(k)]
JOB_NO = {job: n for n, job in enumerate(JOBS)}
LOADS = [job for job in JOBS if job[0:2] != ("qk", 0)]
LOAD_NO = {job: n for n, job in enumerate(LOADS)}


def shift(job, passes):
    if job[0] == "ctx":
        return ("ctx", job[1] + passes * PASS)
    return ("qk", job[1] + passes * (PASS // SJ), job[2])


def linear(i, f):
    if isinstance(i, int):
        return f(i)
    return i * (f(2) - f(1)) + f(1)


def build(nc, x, ctx_n, ctx_t, gamma, beta, w_q, w_kt, w_v, w_out, b_out, gate, Wq, Wk, Wv, Wo, bo,
          W_router, b_router, W1, b1, W2, b2, out):
    with ExitStack() as es:
        def sb(name, shape, dt=F32):
            return es.enter_context(nc.sbuf_tensor(name, shape, dt))

        def sem(name):
            return es.enter_context(nc.semaphore(name))

        qk_dram = nc.dram_tensor("qk_scratch", (B * TPB, P, DT * P), F32, kind="Internal").ap()

        x_sb = sb("x_sb", [P, MT, D])
        ident = sb("ident", [P, P])
        bout_b = sb("bout_b", [P, D])
        bo_b = sb("bo_b", [P, D])
        tg = sb("tg", [P, 2])
        zero = sb("zero", [P, 1])
        mhalf = sb("mhalf", [P, 1])
        stats = sb("stats", [P, MT, 6])
        mv = sb("mv", [P, MT, 2])
        sd = sb("sd", [P, MT])
        rstd = sb("rstd", [P, MT])
        with nc.sbuf_tensor("wv_sb", [P, DT, H * DH], F32) as wv_sb, \
                nc.sbuf_tensor("wout_sb", [P, TPB, D], F32) as wout_sb:
            pass
        h_hi = sb("h_hi", [P, FT, TOK], F32R)
        with nc.sbuf_tensor("wkt_sb", [P, TPB, D], F32) as wkt_sb:
            pass
        with nc.sbuf_tensor("oT", [P, TPB, TOK], F32) as oT:
            pass
        h_lo = sb("h_lo", [P, FT, TOK], F32R)
        stage = oT[:].rearrange("p t (a f) -> p (t a) f", f=2 * P).rearrange("p (s b) f -> p s b f", s=2)
        wo_sb = sb("wo_sb", [P, HP, D])
        wr_sb = sb("wr_sb", [P, DT, NE])
        br_b = sb("br_b", [P, NE])
        b1_sb = sb("b1_sb", [P, NE, FT])
        b2_sb = sb("b2_sb", [NE, D])
        bmask = sb("bmask", [P, P])
        eidx = sb("eidx", [P, NE])
        lmax = sb("lmax", [P, MT, 2, LH])
        lsum = sb("lsum", [P, MT, 2, LH])
        lrec = sb("lrec", [P, MT, 2, LH])
        logit = sb("logit", [P, MT, NE])
        top = sb("top", [P, MT, 8])
        topi = sb("topi", [P, MT, 8], U32)
        topf = sb("topf", [P, MT, 2])
        tdiff = sb("tdiff", [P, MT])
        texp = sb("texp", [P, MT])
        tsum = sb("tsum", [P, MT])
        tw = sb("tw", [P, MT, 2])
        sel = sb("sel", [P, MT, NE])
        gw = sb("gw", [P, MT, NE])
        gwT = sb("gwT", [NE, TOK])
        score_scope = ExitStack()

        def ssb(name, shape):
            return score_scope.enter_context(nc.sbuf_tensor(name, shape, F32R))

        ct_hi = ssb("ct_hi", [P, DT, S])
        ct_lo = ssb("ct_lo", [P, DT, S])
        qk_hi = ssb("qk_hi", [P, 2, DT, GW])
        qk_lo = ssb("qk_lo", [P, 2, DT, GW])
        score_scope.close()
        chain_scope = ExitStack()

        def csb(name, shape):
            return chain_scope.enter_context(nc.sbuf_tensor(name, shape, F32))

        lw_sb = csb("lw_sb", [P, 3, DT, HID])
        ln_out = csb("ln_out", [P, 2, D])
        lnT = csb("lnT", [P, 2, DT, P])
        ke = csb("ke", [P, 2, HP, P])
        qe = csb("qe", [P, 2, HID])
        kn = csb("kn", [P, 2, HID])
        v_sb = csb("v_sb", [P, 2, HID])
        cbd = csb("cbd", [P, 2, 2, HP, P])
        lqT = ke
        lo_T = qe[:].rearrange("p r (t q) -> p r t q", q=P)
        chain_scope.close()
        for n, size in enumerate((DT * S, DT * S, 2 * DT * GW, 2 * DT * GW)):
            sb(f"score_place{n}", [P, size])
        with nc.sbuf_tensor("raw", [P, RR, DT, P], F32) as raw:
            pass
        lnT_hi = sb("lnT_hi", [P, DT, TOK], F32R)
        with nc.sbuf_tensor("cmax", [P, 2, GW], F32) as cmax:
            pass
        lnT_lo = sb("lnT_lo", [P, DT, TOK], F32R)
        mtouch = sb("mtouch", [P, 1])
        rsum = sb("rsum", [P, GT])
        with nc.sbuf_tensor("u_sb", [P, GT, D], F32) as u_sb:
            pass
        h_f = sb("h_f", [P, 2, TOK])
        with nc.sbuf_tensor("xnT", [P, DT, TOK], F32) as xnT:
            pass
        ut_sb = sb("ut_sb", [P, GT, DT, P])
        loop_scope = ExitStack()

        def lsb(name, shape, dt=F32):
            return loop_scope.enter_context(nc.sbuf_tensor(name, shape, dt))

        cn = lsb("cn", [P, SJ, CNW], F32R)
        pro_scope = ExitStack()

        def psb(name, shape, dt=F32):
            return pro_scope.enter_context(nc.sbuf_tensor(name, shape, dt))

        wq_sb = psb("wq_sb", [P, DT, H * DH])
        wkt_hi = psb("wkt_hi", [P, 2, TPB, D], F32R)
        wkt_lo = psb("wkt_lo", [P, 2, TPB, D], F32R)
        qT_hi = psb("qT_hi", [P, TPB, TOK], F32R)
        qT_lo = psb("qT_lo", [P, TPB, TOK], F32R)
        xn = psb("xn", [P, MT, D])
        gamma_c = psb("gamma_c", [P, DT])
        beta_c = psb("beta_c", [P, DT])
        pro_scope.close()
        st = lsb("st", [P, 2, SJ, GW])
        mbc = lsb("mbc", [P, 2, GW])
        pt_hi = lsb("pt_hi", [P, PR, GW], F32R)
        pt_lo = lsb("pt_lo", [P, PR, GW], F32R)
        loop_scope.close()
        tail = ExitStack()

        def tsb(name, shape, dt=F32):
            return tail.enter_context(nc.sbuf_tensor(name, shape, dt))

        w1_hi = tsb("w1_hi", [P, 2, DT, FF], F32R)
        w1_lo = tsb("w1_lo", [P, 2, DT, FF], F32R)
        w2_sp = tsb("w2_sp", [P, 2, FT, 2 * D], F32R)
        w1_raw = tsb("w1_raw", [P, 2, DT, FF])
        w2_raw = tsb("w2_raw", [P, 2, FT, D])
        tail.close()

        sps = es.enter_context(nc.psum_tensor("sps", [P, 2, 512], F32))
        scp = es.enter_context(nc.psum_tensor("scp", [P, GT, 512], F32))
        wps = es.enter_context(nc.psum_tensor("wps", [P, 2, 512], F32))
        trp = [sps[:, 0, :], sps[:, 1, :]]
        up, wp = wps[:, 0, :], wps[:, 1, :]

        x_in = sem("x_in")
        small_in = sem("small_in")
        pw_in = sem("pw_in")
        wkt_in = sem("wkt_in")
        wkt_hi_ok = sem("wkt_hi_ok")
        pad_ok = sem("pad_ok")
        wkt_lo_ok = sem("wkt_lo_ok")
        tw_in = sem("tw_in")
        lw_in = sem("lw_in")
        raw_in = [sem(f"raw_in{i}") for i in range(RR)]
        qk_out = [sem(f"qk_out{i}") for i in range(2)]
        ident_ok = sem("ident_ok")
        pool_step = sem("pool_step")
        split_hi = sem("split_hi")
        ones_ok = sem("ones_ok")
        split_ok = sem("split_ok")
        dve_step = sem("dve_step")
        var_ok = sem("var_ok")
        sd_ok = sem("sd_ok")
        xn_ok = sem("xn_ok")
        pro_tr = sem("pro_tr")
        pro_trc = sem("pro_trc")
        pro_q = sem("pro_q")
        pro_qh = sem("pro_qh")
        pro_ql = sem("pro_ql")
        pro_k = sem("pro_k")
        pro_kc_act = sem("pro_kc_act")
        pro_kc_dve = sem("pro_kc_dve")
        scores_ok = sem("scores_ok")
        out_ok = sem("out_ok")
        max_ok = sem("max_ok")
        mbc_ok = sem("mbc_ok")
        sub_ok = sem("sub_ok")
        exp_ok = sem("exp_ok")
        hi_ok = sem("hi_ok")
        lo_ok = sem("lo_ok")
        pv_ok = sem("pv_ok")
        rsum_ok = sem("rsum_ok")
        u_ok = sem("u_ok")
        ut_ok = sem("ut_ok")
        utc_ok = sem("utc_ok")
        wv_ok = sem("wv_ok")
        o_ok = sem("o_ok")
        tanh_ok = sem("tanh_ok")
        chain_pe = [sem(f"chain_pe{m}") for m in range(MT)]
        chain_act = [sem(f"chain_act{m}") for m in range(MT)]
        chain_dve = [sem(f"chain_dve{m}") for m in range(MT)]
        chain_pool = [sem(f"chain_pool{m}") for m in range(MT)]
        mask_ok = sem("mask_ok")
        eidx_ok = sem("eidx_ok")
        gates_pe = sem("gates_pe")
        gwT_ok = sem("gwT_ok")
        b2_added = sem("b2_added")
        w1_in = [sem(f"w1_in{i}") for i in range(2)]
        w2_in = [sem(f"w2_in{i}") for i in range(2)]
        whi_ok = sem("whi_ok")
        w_ready = sem("w_ready")
        h_ok = sem("h_ok")
        hf_ok = sem("hf_ok")
        hh_ok = sem("hh_ok")
        hl_ok = sem("hl_ok")
        y_ok = sem("y_ok")
        y_stage = sem("y_stage")
        yc_ok = sem("yc_ok")
        stored = sem("stored")

        head_rows = (slice(0, Q), slice(Q, P))

        def chains_in(k, odd):
            return [m for m in range(odd, MT, 2) if 0 <= k - CHAIN_AT[m] < CHAIN_LEN]

        def fixed(v):
            return isinstance(v, int) and v <= 0

        def wait(eng, s, v):
            if not fixed(v):
                eng.wait_ge(s, v)

        def chain_bank(m):
            return [trp[0], trp[1], trp[0], scp[:, MT - 1, :]][m]

        def w_quarter(s, part):
            if part < DT:
                return w1_raw[:, s, part, :], w1_hi[:, s, part, :], w1_lo[:, s, part, :]
            fs = slice((part - DT) * FT // 2, (part - DT + 1) * FT // 2)
            return w2_raw[:, s, fs, :], w2_sp[:, s, fs, 0:D], w2_sp[:, s, fs, D:2 * D]

        def h_cols(p):
            if not isinstance(p, int) or p >= 2:
                return slice(0, TOK)
            return (slice(0, (MT - 1) * P), slice((MT - 1) * P, TOK))[p]

        def small_h(f):
            return slice((f % (FT // 2)) * P, (f % (FT // 2) + 1) * P)

        def tiles(p):
            if not isinstance(p, int) or p >= 2:
                return range(MT)
            return (range(MT - 1), range(MT - 1, MT))[p]

        def tile_no(p, m):
            return m if isinstance(p, int) and p < 2 else (p - 1) * MT + m

        def hbank(f):
            return [trp[0], trp[1], up, wp][f % 4]

        def b1_ap(i, s, f):
            if isinstance(i, int):
                e = i * 2 + s
                return b1_sb[:, e, f:f + 1]
            return b1_sb[:].rearrange("p e f -> p (e f)")[:, bass.ds(i * (2 * FT) + (s * FT + f), 1)]

        block = es.enter_context(nc.Block())

        @block.sync
        def _(sp):
            for m in range(MT):
                sp.dma_start(x_sb[:, m, :], x[P * m:P * (m + 1), :]).then_inc(x_in, 16)
            sp.dma_start(gamma_c[:], gamma).then_inc(small_in, 16)
            sp.dma_start(beta_c[:], beta).then_inc(small_in, 16)
            sp.dma_start(wq_sb[:], w_q.rearrange("(t p) n -> p t n", p=P)).then_inc(pw_in, 16)
            sp.dma_start(wkt_sb[:], w_kt.rearrange("(t p) n -> p t n", p=P)).then_inc(wkt_in, 16)

            def load_ctx_t(count, r, b, j):
                wait(sp, split_ok, count)
                w = P if j < SJ - 1 else SL
                src = ctx_t[b, :, P * j:P * j + w].rearrange("(t p) s -> p t s", p=P)
                sp.dma_start(raw[:, r, :, 0:w], src).then_inc(raw_in[r], 16)

            ctx_rows = ctx_n.rearrange("b s d -> (b s) d")

            def load_ctx(count, r, b, j):
                wait(sp, split_ok, count)
                w = P if j < SJ - 1 else SL
                sp.dma_start(raw[0:w, r, :, :].rearrange("p t f -> p (t f)"),
                             ctx_rows[bass.ds(b * S + P * j, w), :]).then_inc(raw_in[r], 16)

            def load_qk(count, r, n):
                wait(sp, split_ok, count)
                sp.dma_start(raw[:, r, :, :].rearrange("p t f -> p (t f)"), qk_dram[n, :, :]).then_inc(raw_in[r], 16)

            def load_job(job, i):
                no = lambda q: LOAD_NO[shift(job, q)]
                count = linear(i, lambda q: JOB_NO[LOADS[no(q) - RR]] + 1 if no(q) >= RR else 0)
                r = no(1 if not isinstance(i, int) else i) % RR
                if job[0] == "ctx":
                    b = linear(i, lambda q: shift(job, q)[1] // (2 * SJ))
                    c, j = job[1] // SJ, job[1] % SJ
                    (load_ctx if c % 2 else load_ctx_t)(count, r, b, j)
                else:
                    load_qk(count, r, linear(i, lambda q: shift(job, q)[1] * GT + job[2]))

            for job in FIRST_JOBS[0:2 * (SJ - GT)]:
                load_job(job, 0)
            qk_v = qk_dram.rearrange("(b t) p f -> t p b f", t=TPB)
            for t in range(TPB):
                sp.wait_ge(pro_kc_act, 2 * (t + 1))
                sp.wait_ge(pro_kc_dve, 2 * (t + 1))
                b0 = 1 if t < GT else 0
                sp.dma_start(qk_v[t, :, b0:B, :], stage[:, t % 2, b0:B, :]).then_inc(qk_out[t % 2], 16)
                if t >= GT:
                    for job in LATE_LOADS[t - GT]:
                        load_job(job, 0)
            for i in range(2):
                sp.wait_ge(qk_out[i], 16 * TPB // 2)

            def load_weights():
                sp.dma_start(wv_sb[:], w_v.rearrange("(t p) n -> p t n", p=P)).then_inc(tw_in, 16)
                sp.dma_start(wout_sb[:], w_out.rearrange("(t p) n -> p t n", p=P)).then_inc(tw_in, 16)
                sp.dma_start(wo_sb[:], Wo.rearrange("(t p) n -> p t n", p=P)).then_inc(tw_in, 16)
                sp.dma_start(wr_sb[:], W_router.rearrange("(t p) n -> p t n", p=P)).then_inc(tw_in, 16)
                sp.dma_start(br_b[:], b_router.partition_broadcast(P)).then_inc(tw_in, 16)
                sp.dma_start(bout_b[:], b_out.partition_broadcast(P)).then_inc(tw_in, 16)
                sp.dma_start(bo_b[:], bo.partition_broadcast(P)).then_inc(tw_in, 16)
                sp.dma_start(tg[:, 0:1], gate.partition_broadcast(P)).then_inc(tw_in, 16)
                sp.dma_start(b1_sb[:], b1).then_inc(tw_in, 16)
                sp.dma_start(b2_sb[:], b2).then_inc(tw_in, 16)

            def load_pass(i, of):
                for u in range(PASS):
                    if of == 0 and u == SJ:
                        load_weights()
                    for job in slot_jobs(of * PASS + u):
                        load_job(shift(job, -of), i)

            load_pass(0, 0)
            with sp.Fori(0, NPASS - 2) as i:
                load_pass(i, 1)
            load_pass(NPASS - 1, NPASS - 1)

            sp.wait_ge(scores_ok, NSLOT)
            for i, w in ((1, Wk), (0, Wq), (2, Wv)):
                sp.dma_start(lw_sb[:, i, :, :], w.rearrange("(t p) n -> p t n", p=P)).then_inc(lw_in, 16)
            sp.wait_ge(pv_ok, NSLOT)

            def load_expert(e, i, s):
                wait(sp, w_ready, (i * 2 + s - 1) * 4)
                sp.dma_start(w1_raw[:, s, :, :], W1[e].rearrange("(t p) n -> p t n", p=P)).then_inc(w1_in[s], 16)
                sp.dma_start(w2_raw[:, s, :, :], W2[e].rearrange("(t p) n -> p t n", p=P)).then_inc(w2_in[s], 16)

            load_expert(0, 0, 0)
            load_expert(1, 0, 1)
            with sp.Fori(1, NE // 2) as i:
                load_expert(i * 2, i, 0)
                load_expert(i * 2 + 1, i, 1)
            for m in range(MT):
                sp.wait_ge(yc_ok, (NE - 1) * MT + m + 1)
                sp.dma_start(out[P * m:P * (m + 1), :], x_sb[:, m, :]).then_inc(stored, 16)
            sp.wait_ge(stored, 16 * MT)

        @block.gpsimd
        def _(pool):
            steps = [0]

            def link(ins):
                steps[0] += 1
                ins.then_inc(pool_step, 1)
                pool.wait_ge(pool_step, steps[0])

            link(pool.memset(ident[:], 0.0))
            link(pool.memset(zero[:], 0.0))
            link(pool.memset(mhalf[:], -0.5))
            pool.affine_select(out=ident[:], in_=ident[:], compare_op=ALU.not_equal, fill=1.0, base=0,
                               pattern=[[-1, P]], channel_multiplier=1).then_inc(ident_ok, 1)
            for j in range(SJ):
                last = pool.memset(cn[:, j, D:D + 2].bitcast(F32), 1.0)
            last.then_inc(ones_ok, 1)
            pool.iota(eidx[:], pattern=[[1, NE]], base=0, channel_multiplier=0,
                      allow_small_or_imprecise_dtypes=True).then_inc(eidx_ok, 1)
            link(pool.memset(bmask[:], 0.0))
            link(pool.memset(bmask[0:Q, 0:Q], 1.0))
            pool.memset(bmask[Q:P, Q:P], 1.0).then_inc(mask_ok, 1)
            pool.wait_ge(mask_ok, 1)

            def split(src, hi, lo, hi_count, done):
                z = zero[0:src.shape[0], :]
                for _ in range(len(src.shape) - 2):
                    z = z.unsqueeze(1)
                pool.tensor_tensor(hi, src, z.broadcast_to(tuple(src.shape)), ALU.add).then_inc(split_hi, 1)
                pool.wait_ge(split_hi, hi_count + 1)
                pool.tensor_tensor(lo, src, hi.bitcast(F32), ALU.subtract).then_inc(done, 1)

            def split_job(job, i):
                no = linear(i, lambda q: JOB_NO[shift(job, q)])
                if job[0] == "qk" and isinstance(i, int) and shift(job, i)[1] == 0:
                    t = job[2]
                    pool.wait_ge(pro_kc_act, DT * (t + 1))
                    pool.wait_ge(pro_kc_dve, DT * (t + 1))
                    cols = slice(t * P, (t + 1) * P)
                    split(stage[:, t % 2, 0, :].rearrange("p (d q) -> p d q", d=DT),
                          qk_hi[:, 0, :, cols], qk_lo[:, 0, :, cols], no, split_ok)
                    return
                r = LOAD_NO[shift(job, 1 if not isinstance(i, int) else i)] % RR
                pool.wait_ge(raw_in[r], linear(i, lambda q: (LOAD_NO[shift(job, q)] // RR + 1) * 16))
                if job[0] == "qk":
                    wait(pool, scores_ok, linear(i, lambda q: (shift(job, q)[1] - 1) * SJ))
                    slot = job[1] % 2
                    cols = slice(job[2] * P, (job[2] + 1) * P)
                    split(raw[:, r, :, :], qk_hi[:, slot, :, cols], qk_lo[:, slot, :, cols], no, split_ok)
                    return
                j = job[1] % SJ
                w = P if j < SJ - 1 else SL
                if job[1] // SJ % 2 == 0:
                    wait(pool, scores_ok, linear(i, lambda q: shift(job, q)[1] - SJ + 1))
                    cols = slice(P * j, P * j + w)
                    split(raw[:, r, :, 0:w], ct_hi[:, :, cols], ct_lo[:, :, cols], no, split_ok)
                else:
                    wait(pool, pv_ok, linear(i, lambda q: shift(job, q)[1] - 2 * SJ + 1))
                    src = raw[0:w, r, :, :].rearrange("p t f -> p (t f)")
                    split(src, cn[0:w, j, 0:D], cn[0:w, j, D + 2:CNW], no, split_ok)

            def all_max(g, par):
                pool.wait_ge(max_ok, (g + 1) * SJ)
                pool.tensor_tensor(mtouch[:], cmax[:, par, 0:1], zero[:], ALU.add)
                pool.partition_all_reduce(mbc[:, par, :], cmax[:, par, :], P, bass.bass_isa.ReduceOp.max)\
                    .then_inc(mbc_ok, 1)

            def split_pass(i, of):
                for u in range(PASS):
                    if u % SJ == 0 and not (of == 0 and u == 0):
                        all_max(linear(i, lambda q: q * (PASS // SJ) + u // SJ - 1), (u // SJ - 1) % 2)
                    for job in slot_jobs(of * PASS + u):
                        split_job(shift(job, -of), i)

            for job in FIRST_JOBS:
                split_job(job, 0)
            split_pass(0, 0)
            with pool.Fori(0, NPASS - 2) as i:
                split_pass(i, 1)
            split_pass(NPASS - 1, NPASS - 1)
            all_max(NG - 1, (NG - 1) % 2)

            def chain_rstd(m, which):
                pool.wait_ge(chain_dve[m], DVE_NO[("eps1", "eps2")[which - 1]])
                pool.tensor_tensor(rstd[:, m:m + 1], mv[:, m, 1:2], mhalf[:], ALU.pow).then_inc(chain_pool[m], 1)

            def low_weights(i, s, part):
                raw_w, hi, lo = w_quarter(s, part)
                pool.wait_ge(whi_ok, (i * 2 + s) * 4 + part + 1)
                pool.tensor_tensor(lo, raw_w, hi.bitcast(F32), ALU.subtract).then_inc(w_ready, 1)

            for m, which in ((0, 1), (1, 1), (0, 2), (2, 1), (1, 2), (3, 1), (2, 2)):
                chain_rstd(m, which)
            for part in range(4):
                low_weights(0, 0, part)
            low_weights(0, 1, 0)
            chain_rstd(3, 2)
            for part in range(1, 4):
                low_weights(0, 1, part)
            with pool.Fori(1, NE // 2) as i:
                for s in range(2):
                    for part in range(4):
                        low_weights(i, s, part)

        @block.scalar
        def _(act):
            for r in range(2):
                act.wait_ge(var_ok, r + 1)
                act.activation(sd[:], mv[:, :, 1], ACT.Sqrt).then_inc(sd_ok, 1)
            act.wait_ge(wkt_in, 16)
            for x in range(4):
                ts_ = slice(x * TPB // 4, (x + 1) * TPB // 4)
                for par, rows in enumerate(head_rows):
                    act.activation(wkt_hi[rows, par, ts_, :], wkt_sb[rows, ts_, :], ACT.Copy).then_inc(wkt_hi_ok, 1)
            for t in range(TPB):
                act.wait_ge(pro_q, t + 1)
                act.activation(qT_hi[:, t, :], scp[:, t % GT, :], ACT.Copy,
                               scale=float(DH) ** -0.5).then_inc(pro_qh, 1)
            for t in range(TPB):
                if t >= 2:
                    act.wait_ge(qk_out[t % 2], 16 * (t // 2))
                    if t < GT + 2:
                        act.wait_ge(split_ok, JOB_NO[("qk", 0, t - 2)] + 1)
                for dt in range(DT):
                    act.wait_ge(pro_k, DT * t + dt + 1)
                    act.activation(stage[:, t % 2, :, dt * P:dt * P + Q],
                                   scp[:, 2 * dt, :].rearrange("p (b q) -> p b q", q=Q),
                                   ACT.Copy).then_inc(pro_kc_act, 1)

            def rows(j):
                return P if j < SJ - 1 else SL

            def take_scores(i, u):
                j, par = u % SJ, u // SJ % 2
                act.wait_ge(scores_ok, linear(i, lambda q: q * PASS + u + 1))
                act.activation(st[0:rows(j), par, j, :], sps[0:rows(j), u % 2, :], ACT.Copy).then_inc(out_ok, 1)

            def exps(i, u):
                j, par, r = u % SJ, u // SJ % 2, u % PR
                p = st[0:rows(j), par, j, :]
                act.wait_ge(sub_ok, linear(i, lambda q: q * PASS + u + 1))
                act.activation(p, p, ACT.Exp).then_inc(exp_ok, 1)
                act.wait_ge(exp_ok, linear(i, lambda q: q * PASS + u + 1))
                wait(act, pv_ok, linear(i, lambda q: q * PASS + u - PR + 1))
                act.activation(pt_hi[0:rows(j), r, :], p, ACT.Copy).then_inc(hi_ok, 1)

            def take_ut(i, u):
                for x in range(2):
                    act.wait_ge(ut_ok, linear(i, lambda q: (q * (PASS // SJ) + u // SJ - 2) * 2 + x + 1))
                    if x == 0:
                        wait(act, wv_ok, linear(i, lambda q: q * (PASS // SJ) + u // SJ - 2))
                    act.activation(ut_sb[:, 2 * x:2 * x + 2, :, :],
                                   wps[:, x, :].rearrange("p (a t q) -> p a t q", a=2, t=DT), ACT.Copy).then_inc(utc_ok, 1)

            def slot(i, u, k):
                if 1 <= k <= NSLOT:
                    take_scores(i, u - 1)
                if L_SUB <= k < NSLOT + L_SUB:
                    exps(i, u - L_SUB)
                if u % SJ == V_UTC and k >= 2 * SJ:
                    take_ut(i, u)

            for u in range(PASS):
                slot(0, u, u)
            with act.Fori(0, NPASS - 1) as i:
                for u in range(PASS):
                    slot(i, u, PASS + u)
            def chain(m, o):
                r, bank = m % 2, chain_bank(m)

                def after_pe(name):
                    act.wait_ge(chain_pe[m], PE_NO[name])

                def after_dve(name):
                    act.wait_ge(chain_dve[m], DVE_NO[name])

                if o == 2:
                    after_pe("T1")
                    act.activation(lnT[:, r, :, :], bank[:, 0:D].rearrange("p (t q) -> p t q", q=P),
                                   ACT.Copy).then_inc(chain_act[m], 1)
                elif o == 4:
                    after_dve("ksub")
                    act.activation(ke[:, r, :, :], ke[:, r, :, :], ACT.Exp).then_inc(chain_act[m], 1)
                elif o == 5:
                    after_dve("qsub")
                    act.activation(qe[:, r, :], qe[:, r, :], ACT.Exp).then_inc(chain_act[m], 1)
                    after_pe("V")
                    act.activation(v_sb[:, r, :], bank, ACT.Copy).then_inc(chain_act[m], 1)
                elif o == 6:
                    after_pe("KT")
                    act.activation(kn[:, r, :], bank, ACT.Copy).then_inc(chain_act[m], 1)
                elif o == 7:
                    after_pe("QT")
                    act.activation(lqT[:, r, :, :].rearrange("p t q -> p (t q)"), bank,
                                   ACT.Copy).then_inc(chain_act[m], 1)
                elif o == 10:
                    after_pe("OT")
                    act.activation(lo_T[:, r, :, :].rearrange("p t q -> p (t q)"), bank,
                                   ACT.Copy).then_inc(chain_act[m], 1)
                elif o == 13:
                    after_pe("T2")
                    ps = bank[:, 0:D].rearrange("p (t q) -> p t q", q=P)
                    if m == 0:
                        act.wait_ge(split_ok, len(JOBS))
                    act.activation(lnT_hi[:, :, m * P:(m + 1) * P], ps, ACT.Copy).then_inc(chain_act[m], 1)
                    act.activation(lnT[:, r, :, :], ps, ACT.Copy).then_inc(chain_act[m], 1)
                elif o == 15:
                    after_dve("diff")
                    act.activation(texp[:, m:m + 1], tdiff[:, m:m + 1], ACT.Exp).then_inc(chain_act[m], 1)

            def high_weights(i, s, part):
                raw_w, hi, _ = w_quarter(s, part)
                act.wait_ge(w1_in[s] if part < DT else w2_in[s], 16 * (i + 1))
                wait(act, y_ok, (i * 2 + s) * FT if not (isinstance(i, int) and i == 0) else 0)
                act.activation(hi, raw_w, ACT.Copy).then_inc(whi_ok, 1)

            def relu(i, s, p, f):
                c = h_cols(p)
                act.wait_ge(h_ok, p * FT + (f + 1))
                wait(act, hl_ok, p * FT + (f - 1))
                act.activation(h_f[:, f % 2, c], hbank(f)[:, c], ACT.Relu, bias=b1_ap(i, s, f)).then_inc(hf_ok, 1)

            act.wait_ge(tw_in, 16 * NTW)
            act.activation(tg[:, 1:2], tg[:, 0:1], ACT.Tanh).then_inc(tanh_ok, 1)
            for k in range(NSLOT, SPREAD):
                for m in chains_in(k, 1):
                    chain(m, k - CHAIN_AT[m])
                if k < DRAIN:
                    slot(0, k, k)
                for m in chains_in(k, 0):
                    chain(m, k - CHAIN_AT[m])
                if k - W_HI_AT in range(4):
                    high_weights(0, 0, k - W_HI_AT)
            for n in range(2 * FT):
                if n < FT:
                    relu(0, 0, 0, n)
                if n in LAST:
                    chain(MT - 1, LAST[n])
                if n % 4 == 2:
                    high_weights(0, 1, n // 4)
            chain(MT - 1, 15)
            for f in range(FT):
                x = f // (FT // 2)
                if f % (FT // 2) == 0:
                    act.wait_ge(h_ok, FT + (x + 1) * (FT // 2))
                    act.wait_ge(hl_ok, FT)
                act.activation(h_f[:, x, small_h(f)], hbank(x)[:, small_h(f)], ACT.Relu,
                               bias=b1_ap(0, 0, f)).then_inc(hf_ok, 1)

            def experts(i, s, nxt):
                for f in range(FT):
                    relu(i, s, i * 2 + (s + 1), f)
                    if f % 2 and nxt:
                        high_weights(*nxt, f // 2)

            experts(0, 1, (1, 0))
            with act.Fori(1, NE // 2 - 1) as i:
                experts(i, 0, (i, 1))
                experts(i, 1, (i + 1, 0))
            experts(NE // 2 - 1, 0, (NE // 2 - 1, 1))
            experts(NE // 2 - 1, 1, None)

        @block.vector
        def _(dve):
            steps = [0]

            def step(ins):
                steps[0] += 1
                ins.then_inc(dve_step, 1)
                return steps[0]

            dve.memset(wkt_hi[Q:P, 0, :, :].bitcast(F32), 0.0).then_inc(pad_ok, 1)
            dve.wait_ge(x_in, 16 * MT)
            normed = None
            for r in range(2):
                src = x_sb if r == 0 else xn
                collected = []
                for m in range(MT):
                    if r == 1:
                        dve.wait_ge(dve_step, normed[m])
                    collected.append(step(dve.bn_stats(stats[:, m, :], src[:, m, :])))
                for m in range(MT):
                    dve.wait_ge(dve_step, collected[m])
                    last = step(dve.bn_aggr(mv[:, m, :], stats[:, m, :]))
                dve.wait_ge(dve_step, last)
                dve.tensor_scalar(mv[:, :, 1], mv[:, :, 1], EPS, None, ALU.add).then_inc(var_ok, 1)
                dve.wait_ge(sd_ok, r + 1)
                dve.wait_ge(dve_step, step(dve.reciprocal(rstd[:], sd[:])))
                normed = []
                for m in range(MT):
                    ins = dve.tensor_scalar(xn[:, m, :], src[:, m, :], mv[:, m, 0:1], rstd[:, m:m + 1],
                                            ALU.subtract, ALU.mult)
                    if r == 0:
                        normed.append(step(ins))
                    else:
                        ins.then_inc(xn_ok, 1)
            dve.wait_ge(small_in, 32)
            for dt in range(DT):
                dve.wait_ge(pro_tr, dt + 1)
                dve.tensor_scalar(xnT[:, dt, :], trp[dt], gamma_c[:, dt:dt + 1], beta_c[:, dt:dt + 1],
                                  ALU.mult, ALU.add).then_inc(pro_trc, 1)
            dve.memset(wkt_hi[0:Q, 1, :, :].bitcast(F32), 0.0).then_inc(pad_ok, 1)
            for par in range(2):
                dve.memset(wkt_lo[head_rows[1 - par], par, :, :].bitcast(F32), 0.0).then_inc(pad_ok, 1)
            for t in range(TPB):
                dve.wait_ge(pro_qh, t + 1)
                dve.scalar_tensor_tensor(out=qT_lo[:, t, :], in0=scp[:, t % GT, :], scalar=float(DH) ** -0.5,
                                         in1=qT_hi[:, t, :].bitcast(F32), op0=ALU.mult,
                                         op1=ALU.subtract).then_inc(pro_ql, 1)
                if t < 4:
                    ts_ = slice(t * TPB // 4, (t + 1) * TPB // 4)
                    for par, rows in enumerate(head_rows):
                        dve.wait_ge(wkt_hi_ok, 2 * t + par + 1)
                        dve.tensor_tensor(wkt_lo[rows, par, ts_, :], wkt_sb[rows, ts_, :],
                                          wkt_hi[rows, par, ts_, :].bitcast(F32), ALU.subtract).then_inc(wkt_lo_ok, 1)
            for t in range(TPB):
                if t >= 2:
                    dve.wait_ge(qk_out[t % 2], 16 * (t // 2))
                    if t < GT + 2:
                        dve.wait_ge(split_ok, JOB_NO[("qk", 0, t - 2)] + 1)
                for dt in range(DT):
                    dve.wait_ge(pro_k, DT * t + dt + 1)
                    dve.tensor_copy(stage[:, t % 2, :, dt * P + Q:(dt + 1) * P],
                                    scp[:, 2 * dt + 1, :].rearrange("p (b q) -> p b q", q=Q)).then_inc(pro_kc_dve, 1)

            def rows(j):
                return P if j < SJ - 1 else SL

            def minus_max(i, u):
                j, par = u % SJ, u // SJ % 2
                p = st[0:rows(j), par, j, :]
                dve.wait_ge(out_ok, linear(i, lambda q: q * PASS + u + 1))
                if j == 0:
                    dve.wait_ge(mbc_ok, linear(i, lambda q: q * (PASS // SJ) + u // SJ + 1))
                dve.tensor_tensor(p, p, mbc[0:rows(j), par, :], ALU.subtract).then_inc(sub_ok, 1)

            def running_max(i, u):
                j, par = u % SJ, u // SJ % 2
                dve.wait_ge(out_ok, linear(i, lambda q: q * PASS + u + 1))
                src = st[0:rows(j), par, j, :]
                m = cmax[0:rows(j), par, :]
                if j == 0:
                    dve.tensor_copy(m, src).then_inc(max_ok, 1)
                else:
                    dve.wait_ge(max_ok, linear(i, lambda q: q * PASS + u))
                    dve.tensor_tensor(m, m, src, ALU.max).then_inc(max_ok, 1)

            def low_part(i, u):
                j, par, r = u % SJ, u // SJ % 2, u % PR
                dve.wait_ge(hi_ok, linear(i, lambda q: q * PASS + u + 1))
                dve.tensor_tensor(pt_lo[0:rows(j), r, :], st[0:rows(j), par, j, :],
                                  pt_hi[0:rows(j), r, :].bitcast(F32), ALU.subtract).then_inc(lo_ok, 1)

            def take_u(i, u):
                dve.wait_ge(pv_ok, linear(i, lambda q: (q * (PASS // SJ) + u // SJ - 1) * SJ))
                dve.reciprocal(rsum[:].unsqueeze(2), scp[:, :, D:D + 1]).then_inc(rsum_ok, 1)
                wait(dve, ut_ok, linear(i, lambda q: (q * (PASS // SJ) + u // SJ - 2) * 2))
                dve.wait_ge(rsum_ok, linear(i, lambda q: q * (PASS // SJ) + u // SJ - 1))
                for t in range(GT):
                    dve.tensor_scalar(u_sb[:, t, :], scp[:, t, 0:D], rsum[:, t:t + 1], None, ALU.mult).then_inc(u_ok, 1)

            def take_o(i, u, tok):
                half = u // SJ % GPB
                ts_ = slice(half * GT, (half + 1) * GT)
                v = wps[:, 0, :].rearrange("p (t q) -> p t q", t=GT)
                dve.wait_ge(wv_ok, linear(i, lambda q: q * (PASS // SJ) + u // SJ - 1))
                dve.tensor_copy(oT[0:Q, ts_, tok], v[0:Q, :, 0:Q])
                dve.tensor_copy(oT[Q:P, ts_, tok], v[Q:P, :, Q:P]).then_inc(o_ok, 1)

            def slot(i, u, k):
                if L_SUB <= k < NSLOT + L_SUB:
                    minus_max(i, u - L_SUB)
                if L_LO <= k < NSLOT + L_LO:
                    low_part(i, u - L_LO)
                if 1 <= k <= NSLOT:
                    running_max(i, u - 1)
                if u % SJ == V_U and k >= 2 * SJ:
                    take_u(i, u)
                if u % SJ == V_O and k >= 2 * SJ:
                    b = u // (2 * SJ) - 1
                    if isinstance(i, int):
                        take_o(i, u, slice((i * 2 + b) * Q, (i * 2 + b + 1) * Q))
                    else:
                        take_o(i, u, bass.ds(i * (2 * Q) + (b + 2) * Q, Q))

            for u in range(PASS):
                slot(0, u, u)
            with dve.Fori(0, NPASS - 1) as i:
                for u in range(PASS):
                    slot(i, u, PASS + u)
            def chain(m, o):
                r, bank = m % 2, chain_bank(m)
                x_m = x_sb[:, m, :]

                def after_pe(name):
                    dve.wait_ge(chain_pe[m], PE_NO[name])

                def after_act(name):
                    dve.wait_ge(chain_act[m], ACT_NO[name])

                def after(name):
                    dve.wait_ge(chain_dve[m], DVE_NO[name])

                def done(ins):
                    ins.then_inc(chain_dve[m], 1)

                def norm_stats(x_step, a, b):
                    after(x_step)
                    done(dve.bn_stats(stats[:, m, :], x_m))
                    after(a)
                    done(dve.bn_aggr(mv[:, m, :], stats[:, m, :]))
                    after(b)
                    done(dve.tensor_scalar(mv[:, m, 1:2], mv[:, m, 1:2], EPS, None, ALU.add))

                def normalised(which):
                    dve.wait_ge(chain_pool[m], which)
                    done(dve.tensor_scalar(ln_out[:, r, :], x_m, mv[:, m, 0:1], rstd[:, m:m + 1],
                                           ALU.subtract, ALU.mult))

                def heads(ap):
                    return ap.rearrange("p (b n) -> p b n", n=LD)

                def minus_row_max(w, buf, a):
                    done(dve.tensor_reduce(lmax[:, m, w, :], heads(bank), AX.X, ALU.max))
                    after(a)
                    done(dve.tensor_tensor(heads(buf), heads(bank),
                                           lmax[:, m, w, :].unsqueeze(2).broadcast_to((P, LH, LD)), ALU.subtract))

                def normalise(w, buf, a, b):
                    done(dve.tensor_reduce(lsum[:, m, w, :], heads(buf), AX.X, ALU.add))
                    after(a)
                    done(dve.reciprocal(lrec[:, m, w, :], lsum[:, m, w, :]))
                    after(b)
                    done(dve.tensor_tensor(heads(buf), heads(buf),
                                           lrec[:, m, w, :].unsqueeze(2).broadcast_to((P, LH, LD)), ALU.mult))

                ke_m = ke[:, r, :, :].rearrange("p t q -> p (t q)")
                if o == 0:
                    after_pe("O")
                    done(dve.tensor_tensor(ln_out[:, r, :], bank[:, 0:D], bout_b[:], ALU.add))
                    after("o+b")
                    done(dve.scalar_tensor_tensor(out=x_m, in0=ln_out[:, r, :], scalar=tg[:, 1:2], in1=x_m,
                                                  op0=ALU.mult, op1=ALU.add))
                    norm_stats("x1", "stats1", "aggr1")
                elif o == 1:
                    normalised(1)
                elif o == 3:
                    after_pe("K")
                    minus_row_max(0, ke_m, "kmax")
                elif o == 4:
                    after_pe("Q")
                    minus_row_max(1, qe[:, r, :], "qmax")
                    after_act("exp_k")
                    normalise(0, ke_m, "ksum", "krec")
                elif o == 6:
                    after_act("exp_q")
                    normalise(1, qe[:, r, :], "qsum", "qrec")
                elif o in (8, 9):
                    b = o - 8
                    after_pe(("C0", "C1")[b])
                    done(dve.scalar_tensor_tensor(out=cbd[:, r, b, :, :], in0=bank.rearrange("p (t e) -> p t e", e=P),
                                                  scalar=float(LD) ** -0.5,
                                                  in1=bmask[:].unsqueeze(1).broadcast_to((P, HP, P)),
                                                  op0=ALU.mult, op1=ALU.mult))
                elif o == 11:
                    after_pe("Y")
                    done(dve.tensor_tensor(ln_out[:, r, :], bank[:, 0:D], bo_b[:], ALU.add))
                    after("y+b")
                    done(dve.tensor_tensor(x_m, x_m, ln_out[:, r, :], ALU.add))
                    norm_stats("x2", "stats2", "aggr2")
                elif o == 12:
                    normalised(2)
                elif o == 13:
                    after_act("lnT2")
                    cols = slice(m * P, (m + 1) * P)
                    if m == 0:
                        dve.wait_ge(mbc_ok, NG)
                    done(dve.tensor_tensor(lnT_lo[:, :, cols], bank[:, 0:D].rearrange("p (t q) -> p t q", q=P),
                                           lnT_hi[:, :, cols].bitcast(F32), ALU.subtract))
                elif o == 14:
                    after_pe("R")
                    done(dve.tensor_tensor(logit[:, m, :], bank[:, 0:NE], br_b[:], ALU.add))
                    after("logit")
                    done(dve.max(top[:, m, :], logit[:, m, :]))
                    after("top")
                    done(dve.tensor_tensor(tdiff[:, m:m + 1], top[:, m, 1:2], top[:, m, 0:1], ALU.subtract))
                    done(dve.max_index(topi[:, m, :], top[:, m, :], logit[:, m, :]))
                    after("index")
                    done(dve.tensor_copy(topf[:, m, :], topi[:, m, 0:2]))
                elif o == 15:
                    after_act("exp_diff")
                    done(dve.tensor_scalar(tsum[:, m:m + 1], texp[:, m:m + 1], 1.0, None, ALU.add))
                    after("1+e")
                    done(dve.reciprocal(tw[:, m, 0:1], tsum[:, m:m + 1]))
                    after("w0")
                    done(dve.tensor_tensor(tw[:, m, 1:2], tw[:, m, 0:1], texp[:, m:m + 1], ALU.mult))
                    after("w1")
                    done(dve.tensor_scalar(gw[:, m, :], eidx[:], topf[:, m, 0:1], tw[:, m, 0:1],
                                           ALU.is_equal, ALU.mult))
                    done(dve.tensor_scalar(sel[:, m, :], eidx[:], topf[:, m, 1:2], tw[:, m, 1:2],
                                           ALU.is_equal, ALU.mult))
                    after("sel")
                    done(dve.tensor_tensor(gw[:, m, :], gw[:, m, :], sel[:, m, :], ALU.add))
            dve.wait_ge(tanh_ok, 1)
            dve.wait_ge(mask_ok, 1)
            dve.wait_ge(eidx_ok, 1)
            def gate_ap(i, s, m):
                if isinstance(i, int):
                    return gw[:, m, i * 2 + s:i * 2 + s + 1]
                return gw[:].rearrange("p m e -> p (m e)")[:, bass.ds(i * 2 + (m * NE + s), 1)]

            def split_h(p, f):
                c = h_cols(p)
                dve.wait_ge(hf_ok, p * FT + (f + 1))
                wait(dve, y_ok, p * FT + (f + 1 - FT))
                dve.tensor_copy(h_hi[:, f, c], h_f[:, f % 2, c]).then_inc(hh_ok, 1)
                dve.wait_ge(hh_ok, p * FT + (f + 1))
                dve.tensor_tensor(h_lo[:, f, c], h_f[:, f % 2, c], h_hi[:, f, c].bitcast(F32),
                                  ALU.subtract).then_inc(hl_ok, 1)

            def add_y(i, s, p, last=False):
                for m in tiles(p):
                    dve.wait_ge(y_ok, p * FT + (m + 1) * FT // MT if last else (p + 1) * FT)
                    dve.scalar_tensor_tensor(out=x_sb[:, m, :], in0=scp[:, m, 0:D], scalar=gate_ap(i, s, m),
                                             in1=x_sb[:, m, :], op0=ALU.mult, op1=ALU.add).then_inc(y_stage, 1)
                    dve.wait_ge(y_stage, tile_no(p, m) + 1)
                    dve.scalar_tensor_tensor(out=x_sb[:, m, :], in0=scp[:, m, D:2 * D], scalar=gate_ap(i, s, m),
                                             in1=x_sb[:, m, :], op0=ALU.mult, op1=ALU.add).then_inc(yc_ok, 1)

            for k in range(NSLOT, SPREAD):
                for m in chains_in(k, 1):
                    chain(m, k - CHAIN_AT[m])
                if k < DRAIN:
                    slot(0, k, k)
                for m in chains_in(k, 0):
                    chain(m, k - CHAIN_AT[m])
            for n in range(2 * FT):
                if n < FT:
                    split_h(0, n)
                if n in LAST:
                    chain(MT - 1, LAST[n])
            for x in range(2):
                dve.wait_ge(hf_ok, FT + (x + 1) * (FT // 2))
                fs, c = slice(x * (FT // 2), (x + 1) * (FT // 2)), h_cols(1)
                src = h_f[:, x, :].rearrange("p (f q) -> p f q", q=P)
                dve.tensor_copy(h_hi[:, fs, c], src).then_inc(hh_ok, FT // 2)
                dve.wait_ge(hh_ok, FT + (x + 1) * (FT // 2))
                dve.tensor_tensor(h_lo[:, fs, c], src, h_hi[:, fs, c].bitcast(F32),
                                  ALU.subtract).then_inc(hl_ok, FT // 2)
            chain(MT - 1, 15)
            dve.wait_ge(gates_pe, 1)
            dve.tensor_copy(gwT[:], hbank(3)[0:NE, :]).then_inc(gwT_ok, 1)
            add_y(0, 0, 0)
            dve.wait_ge(gates_pe, 2)
            dve.wait_ge(yc_ok, MT - 1)
            for x in range(2):
                dve.tensor_tensor(x_sb[:, 2 * x:2 * x + 2, :], x_sb[:, 2 * x:2 * x + 2, :],
                                  hbank(2 + x).rearrange("p (m d) -> p m d", d=D), ALU.add).then_inc(b2_added, 1)
            dve.wait_ge(b2_added, 2)
            add_y(0, 0, 1)

            def expert(i, s):
                for f in range(FT):
                    split_h(i * 2 + (s + 1), f)
                add_y(i, s, i * 2 + (s + 1), isinstance(i, int) and i * 2 + s == NE - 1)

            expert(0, 1)
            with dve.Fori(1, NE // 2 - 1) as i:
                expert(i, 0)
                expert(i, 1)
            expert(NE // 2 - 1, 0)
            expert(NE // 2 - 1, 1)

        @block.tensor
        def _(pe):
            pe.wait_ge(ident_ok, 1)
            for m in range(MT):
                pe.wait_ge(xn_ok, m + 1)
                for dt in range(DT):
                    ins = pe.transpose(trp[dt][:, m * P:(m + 1) * P], xn[:, m, dt * P:(dt + 1) * P], ident[:])
                    if m == MT - 1:
                        ins.then_inc(pro_tr, 1)
            pe.wait_ge(pw_in, 16)
            for t in range(TPB):
                if t >= GT:
                    pe.wait_ge(pro_ql, t - GT + 1)
                for dt in range(DT):
                    if t == 0:
                        pe.wait_ge(pro_trc, dt + 1)
                    ins = pe.matmul(scp[:, t % GT, :], wq_sb[:, dt, t * P:(t + 1) * P], xnT[:, dt, :],
                                    start=dt == 0, stop=dt == DT - 1)
                ins.then_inc(pro_q, 1)
            pe.wait_ge(wkt_lo_ok, 8)
            pe.wait_ge(pad_ok, 4)
            for t in range(TPB):
                for dt in range(DT):
                    if t == 0:
                        pe.wait_ge(pro_ql, TPB - 2 + 2 * dt)
                    else:
                        pe.wait_ge(pro_kc_act, DT * (t - 1) + dt + 1)
                        pe.wait_ge(pro_kc_dve, DT * (t - 1) + dt + 1)
                    for c, (w, v) in enumerate(((wkt_hi, qT_hi), (wkt_hi, qT_lo), (wkt_lo, qT_hi))):
                        for par in range(2):
                            ins = pe.matmul(scp[:, 2 * dt + par, :], w[:, par, t, dt * P:(dt + 1) * P], v[:, t, :],
                                            start=c == 0, stop=c == 2)
                    ins.then_inc(pro_k, 1)

            def rows(j):
                return P if j < SJ - 1 else SL

            def scores(i, u):
                j, par = u % SJ, u // SJ % 2
                w = 2 * SJ * (u // (2 * SJ)) + j
                need = [("ctx", w)]
                if j == 0:
                    need.append(("qk", u // SJ, GT - 1))
                pe.wait_ge(split_ok, linear(i, lambda q: max(JOB_NO[shift(n, q)] for n in need) + 1))
                wait(pe, out_ok, linear(i, lambda q: q * PASS + u - 1))
                cols = slice(P * j, P * j + rows(j))
                c = 0
                for dt in range(DT):
                    for a, v in ((ct_hi, qk_hi), (ct_hi, qk_lo), (ct_lo, qk_hi)):
                        ins = pe.matmul(sps[0:rows(j), u % 2, :], a[:, dt, cols], v[:, par, dt, :],
                                        start=c == 0, stop=c == 5)
                        c += 1
                ins.then_inc(scores_ok, 1)

            def times_context(i, u):
                j, r = u % SJ, u % PR
                pe.wait_ge(lo_ok, linear(i, lambda q: q * PASS + u + 1))
                w = 2 * SJ * (u // (2 * SJ)) + SJ + j
                pe.wait_ge(split_ok, linear(i, lambda q: JOB_NO[shift(("ctx", w), q)] + 1))
                for t in range(GT):
                    if j == 0:
                        wait(pe, u_ok, linear(i, lambda q: (q * (PASS // SJ) + u // SJ - 1) * GT + t + 1))
                    cols = slice(t * P, (t + 1) * P)
                    hi, lo = pt_hi[0:rows(j), r, cols], pt_lo[0:rows(j), r, cols]
                    pe.matmul(scp[:, t, 0:D + 2], hi, cn[0:rows(j), j, 0:D + 2], start=j == 0, stop=False)
                    pe.matmul(scp[:, t, 0:D], hi, cn[0:rows(j), j, D + 2:CNW], start=False, stop=False)
                    ins = pe.matmul(scp[:, t, 0:D + 2], lo, cn[0:rows(j), j, 0:D + 2], start=False, stop=j == SJ - 1)
                ins.then_inc(pv_ok, 1)

            def transpose_u(i, u):
                for x in range(2):
                    pe.wait_ge(u_ok, linear(i, lambda q: (q * (PASS // SJ) + u // SJ - 2) * GT + 2 * x + 2))
                    if x == 0:
                        wait(pe, o_ok, linear(i, lambda q: q * (PASS // SJ) + u // SJ - 2))
                    for a in range(2):
                        for dt in range(DT):
                            ins = pe.transpose(wps[:, x, (a * DT + dt) * P:(a * DT + dt + 1) * P],
                                               u_sb[:, 2 * x + a, dt * P:(dt + 1) * P], ident[:])
                    ins.then_inc(ut_ok, 1)

            def times_wv(i, u):
                half = u // SJ % GPB
                if isinstance(i, int) and u == 2 * SJ + V_WV:
                    pe.wait_ge(tw_in, 16 * NTW)
                pe.wait_ge(utc_ok, linear(i, lambda q: (q * (PASS // SJ) + u // SJ - 1) * 2))
                for t in range(GT):
                    h0 = (half * GT + t) * P
                    for dt in range(DT):
                        ins = pe.matmul(wps[:, 0, t * P:(t + 1) * P], wv_sb[:, dt, h0:h0 + P], ut_sb[:, t, dt, :],
                                        start=dt == 0, stop=dt == DT - 1)
                ins.then_inc(wv_ok, 1)

            def slot(i, u, k):
                if k < NSLOT:
                    scores(i, u)
                if L_PV <= k < NSLOT + L_PV:
                    times_context(i, u - L_PV)
                if u % SJ == V_UT and k >= 2 * SJ:
                    transpose_u(i, u)
                if u % SJ == V_WV and k >= 2 * SJ:
                    times_wv(i, u)

            pe.wait_ge(ones_ok, 1)
            for u in range(PASS):
                slot(0, u, u)
            with pe.Fori(0, NPASS - 1) as i:
                for u in range(PASS):
                    slot(i, u, PASS + u)
            def chain(m, o):
                r, bank = m % 2, chain_bank(m)
                cols = slice(m * P, (m + 1) * P)

                def after_act(name):
                    pe.wait_ge(chain_act[m], ACT_NO[name])

                def after_dve(name):
                    pe.wait_ge(chain_dve[m], DVE_NO[name])

                def done(ins):
                    ins.then_inc(chain_pe[m], 1)

                if o == 0:
                    pe.wait_ge(o_ok, 4 * (m + 1))
                    if m < 2:
                        pe.wait_ge(out_ok, NSLOT)
                    else:
                        pe.wait_ge(chain_dve[m - 2], DVE_NO["logit"])
                    for t in range(TPB):
                        ins = pe.matmul(bank[:, 0:D], oT[:, t, cols], wout_sb[:, t, :],
                                        start=t == 0, stop=t == TPB - 1)
                    done(ins)
                elif o == 2:
                    after_dve("ln1")
                    for dt in range(DT):
                        ins = pe.transpose(bank[:, dt * P:(dt + 1) * P], ln_out[:, r, dt * P:(dt + 1) * P], ident[:])
                    done(ins)
                elif o == 3:
                    if m == 0:
                        pe.wait_ge(lw_in, 48)
                    after_act("lnT")
                    for t in range(HP):
                        for dt in range(DT):
                            ins = pe.matmul(bank[:, t * P:(t + 1) * P], lw_sb[:, 1, dt, t * P:(t + 1) * P],
                                            lnT[:, r, dt, :], start=dt == 0, stop=dt == DT - 1)
                    done(ins)
                elif o in (4, 5):
                    after_dve("ksub" if o == 4 else "qsub")
                    for dt in range(DT):
                        ins = pe.matmul(bank, lnT[:, r, dt, :], lw_sb[:, 0 if o == 4 else 2, dt, :],
                                        start=dt == 0, stop=dt == DT - 1)
                    done(ins)
                elif o == 6:
                    after_act("v")
                    after_dve("kmul")
                    for t in range(HP):
                        ins = pe.transpose(bank[:, t * P:(t + 1) * P], ke[:, r, t, :], ident[:])
                    done(ins)
                elif o == 7:
                    after_act("kn")
                    after_dve("qmul")
                    for t in range(HP):
                        ins = pe.transpose(bank[:, t * P:(t + 1) * P], qe[:, r, t * P:(t + 1) * P], ident[:])
                    done(ins)
                elif o in (8, 9):
                    b = o - 8
                    if b == 0:
                        after_act("lqT")
                    else:
                        after_dve("cbd0")
                    rows = slice(b * Q, (b + 1) * Q)
                    for t in range(HP):
                        ins = pe.matmul(bank[:, t * P:(t + 1) * P], kn[rows, r, t * P:(t + 1) * P],
                                        v_sb[rows, r, t * P:(t + 1) * P], start=True, stop=True)
                    done(ins)
                elif o == 10:
                    after_dve("cbd1")
                    for t in range(HP):
                        for b in range(2):
                            ins = pe.matmul(bank[:, t * P + b * Q:t * P + (b + 1) * Q], cbd[:, r, b, t, :],
                                            lqT[:, r, t, b * Q:(b + 1) * Q], start=True, stop=True)
                    done(ins)
                elif o == 11:
                    after_act("lo_T")
                    for t in range(HP):
                        ins = pe.matmul(bank[:, 0:D], lo_T[:, r, t, :], wo_sb[:, t, :],
                                        start=t == 0, stop=t == HP - 1)
                    done(ins)
                elif o == 13:
                    after_dve("ln2")
                    for dt in range(DT):
                        ins = pe.transpose(bank[:, dt * P:(dt + 1) * P], ln_out[:, r, dt * P:(dt + 1) * P], ident[:])
                    done(ins)
                elif o == 14:
                    after_act("lnT2")
                    after_dve("lnT_lo")
                    for dt in range(DT):
                        ins = pe.matmul(bank[:, 0:NE], lnT[:, r, dt, :], wr_sb[:, dt, :],
                                        start=dt == 0, stop=dt == DT - 1)
                    done(ins)
            def h_tile(s, p, f, e):
                if f == 0:
                    pe.wait_ge(w_ready, e * 4 + DT)
                if isinstance(p, int) and p == 0:
                    if f == 0:
                        for m in tiles(0):
                            pe.wait_ge(chain_dve[m], DVE_NO["logit"])
                wait(pe, hf_ok, p * FT + (f - 3))
                c, n = h_cols(p), 0
                for dt in range(DT):
                    for w, v in ((w1_hi, lnT_hi), (w1_hi, lnT_lo), (w1_lo, lnT_hi)):
                        ins = pe.matmul(hbank(f)[:, c], w[:, s, dt, f * P:(f + 1) * P], v[:, dt, c],
                                        start=n == 0, stop=n == 5)
                        n += 1
                ins.then_inc(h_ok, 1)

            def y_tile(s, p, f, e):
                if f == 0:
                    pe.wait_ge(w_ready, (e + 1) * 4)
                pe.wait_ge(hl_ok, p * FT + (f + 1))
                for m in tiles(p):
                    if f == 0 and not (isinstance(p, int) and p < 2):
                        wait(pe, yc_ok, tile_no(p, m) - (MT - 1))
                    ms = slice(m * P, (m + 1) * P)
                    pe.matmul(scp[:, m, :], h_hi[:, f, ms], w2_sp[:, s, f, :], start=f == 0, stop=False)
                    ins = pe.matmul(scp[:, m, 0:D], h_lo[:, f, ms], w2_sp[:, s, f, 0:D],
                                    start=False, stop=f == FT - 1)
                ins.then_inc(y_ok, 1)

            def expert(i, s):
                for f in range(FT):
                    h_tile(s, i * 2 + (s + 1), f, i * 2 + s)
                for f in range(FT):
                    y_tile(s, i * 2 + (s + 1), f, i * 2 + s)

            for k in range(NSLOT, SPREAD):
                for m in chains_in(k, 1):
                    chain(m, k - CHAIN_AT[m])
                if k < DRAIN:
                    slot(0, k, k)
                for m in chains_in(k, 0):
                    chain(m, k - CHAIN_AT[m])
            for n in range(2 * FT):
                if n < FT:
                    h_tile(0, 0, n, 0)
                else:
                    y_tile(0, 0, n - FT, 0)
                if n in LAST:
                    chain(MT - 1, LAST[n])
            pe.wait_ge(hf_ok, FT)
            pe.wait_ge(chain_dve[MT - 1], DVE_NO["lnT_lo"])
            for f in range(FT):
                c, n = h_cols(1), 0
                for dt in range(DT):
                    for w, v in ((w1_hi, lnT_hi), (w1_hi, lnT_lo), (w1_lo, lnT_hi)):
                        ins = pe.matmul(hbank(f // (FT // 2))[:, small_h(f)], w[:, 0, dt, f * P:(f + 1) * P],
                                        v[:, dt, c], start=n == 0, stop=n == 5)
                        n += 1
                if f % (FT // 2) == FT // 2 - 1:
                    ins.then_inc(h_ok, FT // 2)
            pe.wait_ge(chain_dve[MT - 1], DVE_NO["logit"])
            for f in range(FT):
                y_tile(0, 1, f, 0)
            pe.wait_ge(chain_dve[MT - 1], DVE_NO["gw"])
            for m in range(MT):
                ins = pe.transpose(hbank(3)[0:NE, m * P:(m + 1) * P], gw[:, m, :], ident[:])
            ins.then_inc(gates_pe, 1)
            pe.wait_ge(hf_ok, 2 * FT)
            h_tile(1, 2, 0, 1)
            pe.wait_ge(gwT_ok, 1)
            for m in range(MT):
                ins = pe.matmul(hbank(2 + m // 2)[:, m % 2 * D:(m % 2 + 1) * D], gwT[:, m * P:(m + 1) * P], b2_sb[:],
                                start=True, stop=True)
            ins.then_inc(gates_pe, 1)
            h_tile(1, 2, 1, 1)
            pe.wait_ge(b2_added, 2)
            for f in range(2, FT):
                h_tile(1, 2, f, 1)
            for f in range(FT):
                y_tile(1, 2, f, 1)
            with pe.Fori(1, NE // 2 - 1) as i:
                expert(i, 0)
                expert(i, 1)
            expert(NE // 2 - 1, 0)
            for f in range(FT):
                h_tile(1, NE, f, NE - 1)
            pe.wait_ge(w_ready, NE * 4)
            for m in range(MT):
                pe.wait_ge(yc_ok, (NE - 1) * MT + m - (MT - 1))
                ms = slice(m * P, (m + 1) * P)
                for f in range(FT):
                    if m == 0:
                        pe.wait_ge(hl_ok, NE * FT + f + 1)
                    pe.matmul(scp[:, m, :], h_hi[:, f, ms], w2_sp[:, 1, f, :], start=f == 0, stop=False)
                    ins = pe.matmul(scp[:, m, 0:D], h_lo[:, f, ms], w2_sp[:, 1, f, 0:D],
                                    start=False, stop=f == FT - 1)
                ins.then_inc(y_ok, FT // MT)


NTW = 10


def number(names):
    return {name: n + 1 for n, name in enumerate(names.split())}


PE_NO = number("O T1 K Q V KT QT C0 C1 OT Y T2 R")
ACT_NO = number("lnT exp_k exp_q v kn lqT lo_T lnT_hi lnT2 exp_diff")
DVE_NO = number("o+b x1 stats1 aggr1 eps1 ln1 kmax ksub qmax qsub ksum krec kmul qsum qrec qmul cbd0 cbd1 "
                "y+b x2 stats2 aggr2 eps2 ln2 lnT_lo logit top diff index topf 1+e w0 w1 gw0 sel gw")


def kernel(**inputs):
    import numpy as np
    import concourse.bacc as bacc
    from concourse.bass_utils import run_bass_kernel_spmd

    a = {k: np.asarray(v) for k, v in inputs.items()}
    inner = H * DH
    w_kv = a["L0_xattn_w_kv"]
    arrays = {
        "x": a["x"].reshape(TOK, D),
        "ctx_n": a["ctx_1024"],
        "ctx_t": a["ctx_1024"].transpose(0, 2, 1),
        "gamma": a["L0_xattn_ln_gamma"].reshape(DT, P).T,
        "beta": a["L0_xattn_ln_beta"].reshape(DT, P).T,
        "w_q": a["L0_xattn_w_q"],
        "w_kt": w_kv[:, :inner].T,
        "w_v": w_kv[:, inner:],
        "w_out": a["L0_xattn_w_out"],
        "b_out": a["L0_xattn_b_out"],
        "gate": a["L0_xattn_gate"],
        "Wq": a["L0_attn_Wq"], "Wk": a["L0_attn_Wk"], "Wv": a["L0_attn_Wv"], "Wo": a["L0_attn_Wo"],
        "bo": a["L0_attn_bo"],
        "W_router": a["L0_ffn_W_router"], "b_router": a["L0_ffn_b_router"],
        "W1": a["L0_ffn_W1"],
        "b1": a["L0_ffn_b1"].reshape(NE, FT, P).transpose(2, 0, 1),
        "W2": a["L0_ffn_W2"],
        "b2": a["L0_ffn_b2"],
    }
    arrays = {k: np.ascontiguousarray(v) for k, v in arrays.items()}
    nc = bacc.Bacc("TRN2", target_bir_lowering=False, num_devices=1)
    args = [nc.dram_tensor(k, v.shape, mybir.dt.from_np(v.dtype), kind="ExternalInput").ap()
            for k, v in arrays.items()]
    out = nc.dram_tensor("out", (TOK, D), F32, kind="ExternalOutput").ap()
    build(nc, *args, out)
    r = run_bass_kernel_spmd(nc, [arrays], core_ids=[0])
    return r.results[0]["out"].reshape(B, Q, D)
```
